# Optimizing a Trainium2 kernel written in Bass

```python
import numpy as np
import jax
import jax.numpy as jnp

def _softmax(x, axis=-1):
    return jax.nn.softmax(x, axis=axis)

def _gelu(x):
    return jax.nn.gelu(x, approximate=True)

def _silu(x):
    return jax.nn.silu(x)

def _sigmoid(x):
    return jax.nn.sigmoid(x)

def _layernorm(x, axis=-1, eps=1e-05):
    m = jnp.mean(x, axis=axis, keepdims=True)
    v = jnp.var(x, axis=axis, keepdims=True)
    return (x - m) / jnp.sqrt(v + eps)

def _scatter_add(tgt, idx, src, axis=0):
    return tgt.at[idx].add(src)

def _segment_sum(src, seg, n):
    return jax.ops.segment_sum(src, seg, n)
kernel_name = 'mk_lm_tower_d1_tok_ids2048_r4_e0c374'

def setup_inputs(seed: int=0):
    np.random.seed(seed)
    _w = jnp.asarray

    def _rec_inputs():
        import jax
        import jax.numpy as jnp
        _rk = jax.random.key(seed)
        x = jax.random.randint(jax.random.fold_in(_rk, 1), (1, 2048), 0, 12564, jnp.int32)
        return x
    x = _rec_inputs()

    def _L0_tok_setup():
        import jax, jax.numpy as jnp
        import numpy as np
        import math
        VOCAB = 50257
        DIM = 512
        R = 64
        SCALING = 128.0 / math.sqrt(R)
        key = jax.random.key(seed)
        k1, k2, k3 = jax.random.split(key, 3)
        x = jax.random.randint(k1, (4, 1024), 0, VOCAB)
        weight = jax.random.normal(k2, (VOCAB, DIM), dtype=jnp.float32)
        lora_A = jax.random.normal(k3, (R, VOCAB), dtype=jnp.float32) / math.sqrt(R)
        lora_B = jax.random.normal(jax.random.fold_in(key, 7), (DIM, R), dtype=jnp.float32) * 0.02
        return {'x': x, 'weight': weight, 'lora_A': lora_A, 'lora_B': lora_B}
    _L0_tok_all = _L0_tok_setup()
    _L0_tok_in = {k: v for k, v in _L0_tok_all.items() if k in ('weight', 'lora_A', 'lora_B')}
    del _L0_tok_all

    def _L0_attn_setup():
        import jax, jax.numpy as jnp
        import numpy as np
        N_HEADS, D_MODEL, D_HEAD, SEQ, BATCH = (16, 512, 128, 512, 1)
        ATTN_SCALE = float(np.sqrt(D_HEAD))
        ROPE_BASE = 10000.0

        def _rope_cos_sin(seq_len, d_head, dtype):
            inv_freq = 1.0 / ROPE_BASE ** (jnp.arange(0, d_head, 2, dtype=jnp.float32) / d_head)
            t = jnp.arange(seq_len, dtype=jnp.float32)
            freqs = t[:, None] * inv_freq[None, :]
            return (jnp.cos(freqs).astype(dtype), jnp.sin(freqs).astype(dtype))

        def _apply_rotary(x, cos, sin):
            B, S, H, D = x.shape
            x2 = x.reshape(B, S, H, D // 2, 2)
            xr, xi = (x2[..., 0], x2[..., 1])
            c = cos[None, :, None, :]
            s = sin[None, :, None, :]
            outr = xr * c - xi * s
            outi = xr * s + xi * c
            return jnp.stack([outr, outi], axis=-1).reshape(B, S, H, D)
        key = jax.random.key(seed)
        ks = jax.random.split(key, 9)
        std = 0.02
        return {'resid_pre': jax.random.normal(ks[0], (BATCH, SEQ, D_MODEL), dtype=jnp.float32), 'W_Q': jax.random.normal(ks[1], (N_HEADS, D_MODEL, D_HEAD), dtype=jnp.float32) * std, 'W_K': jax.random.normal(ks[2], (N_HEADS, D_MODEL, D_HEAD), dtype=jnp.float32) * std, 'W_V': jax.random.normal(ks[3], (N_HEADS, D_MODEL, D_HEAD), dtype=jnp.float32) * std, 'W_O': jax.random.normal(ks[4], (N_HEADS, D_HEAD, D_MODEL), dtype=jnp.float32) * std, 'b_Q': jnp.zeros((N_HEADS, D_HEAD), dtype=jnp.float32), 'b_K': jnp.zeros((N_HEADS, D_HEAD), dtype=jnp.float32), 'b_V': jnp.zeros((N_HEADS, D_HEAD), dtype=jnp.float32), 'b_O': jnp.zeros((D_MODEL,), dtype=jnp.float32)}
    _L0_attn_all = _L0_attn_setup()
    _L0_attn_in = {k: v for k, v in _L0_attn_all.items() if k in ('W_Q', 'W_K', 'W_V', 'W_O', 'b_Q', 'b_K', 'b_V', 'b_O')}
    del _L0_attn_all

    def _L0_ffn_setup():
        import jax, jax.numpy as jnp
        import numpy as np
        E = 32
        K = 8
        H = 512
        F = 192
        B, S = (1, 256)

        def _moe(x, wg, w1, v1, w2):
            T = x.shape[0]
            logits = x @ wg.T
            scores = jax.nn.softmax(logits, axis=-1)
            weights, idx = jax.lax.top_k(scores, K)
            weights = weights / jnp.sum(weights, axis=-1, keepdims=True)
            flat_e = idx.reshape(-1)
            flat_t = jnp.repeat(jnp.arange(T), K)
            flat_w = weights.reshape(-1)
            order = jnp.argsort(flat_e)
            e_s = flat_e[order]
            t_s = flat_t[order]
            w_s = flat_w[order]
            group_sizes = jnp.bincount(e_s, length=E).astype(jnp.int32)
            xs = x[t_s]
            g = jax.lax.ragged_dot(xs, w1, group_sizes)
            u = jax.lax.ragged_dot(xs, v1, group_sizes)
            h = jax.nn.silu(g) * u
            ys = jax.lax.ragged_dot(h, w2, group_sizes)
            out = jnp.zeros((T, x.shape[1]), x.dtype).at[t_s].add(ys * w_s[:, None])
            return out
        key = jax.random.key(seed)
        k0, k1, k2, k3, k4 = jax.random.split(key, 5)
        scale = 0.02
        return {'hidden_states': jax.random.normal(k0, (B, S, H), jnp.float32), 'wg': jax.random.normal(k1, (E, H), jnp.float32) * scale, 'w1': jax.random.normal(k2, (E, H, F), jnp.float32) * scale, 'v1': jax.random.normal(k3, (E, H, F), jnp.float32) * scale, 'w2': jax.random.normal(k4, (E, F, H), jnp.float32) * scale}
    _L0_ffn_all = _L0_ffn_setup()
    _L0_ffn_in = {k: v for k, v in _L0_ffn_all.items() if k in ('wg', 'w1', 'v1', 'w2')}
    del _L0_ffn_all
    return {'x': x, 'L0_tok_weight': _L0_tok_in['weight'], 'L0_tok_lora_A': _L0_tok_in['lora_A'], 'L0_tok_lora_B': _L0_tok_in['lora_B'], 'L0_attn_W_Q': _L0_attn_in['W_Q'], 'L0_attn_W_K': _L0_attn_in['W_K'], 'L0_attn_W_V': _L0_attn_in['W_V'], 'L0_attn_W_O': _L0_attn_in['W_O'], 'L0_attn_b_Q': _L0_attn_in['b_Q'], 'L0_attn_b_K': _L0_attn_in['b_K'], 'L0_attn_b_V': _L0_attn_in['b_V'], 'L0_attn_b_O': _L0_attn_in['b_O'], 'L0_ffn_wg': _L0_ffn_in['wg'], 'L0_ffn_w1': _L0_ffn_in['w1'], 'L0_ffn_v1': _L0_ffn_in['v1'], 'L0_ffn_w2': _L0_ffn_in['w2']}

def reference(x, L0_tok_weight, L0_tok_lora_A, L0_tok_lora_B, L0_attn_W_Q, L0_attn_W_K, L0_attn_W_V, L0_attn_W_O, L0_attn_b_Q, L0_attn_b_K, L0_attn_b_V, L0_attn_b_O, L0_ffn_wg, L0_ffn_w1, L0_ffn_v1, L0_ffn_w2):
    import jax
    import jax.numpy as jnp

    def _L0_tok_ref(x, weight, lora_A, lora_B):
        import jax, jax.numpy as jnp
        import numpy as np
        import math
        VOCAB = 50257
        DIM = 512
        R = 64
        SCALING = 128.0 / math.sqrt(R)
        base_embed = weight[x]
        a_rows = lora_A.T[x]
        lora_embed = jnp.einsum('bsr,dr->bsd', a_rows, lora_B)
        return base_embed + lora_embed * SCALING

    def _L0_attn_ref(resid_pre, W_Q, W_K, W_V, W_O, b_Q, b_K, b_V, b_O):
        import jax, jax.numpy as jnp
        import numpy as np
        N_HEADS, D_MODEL, D_HEAD, SEQ, BATCH = (16, 512, 128, 512, 1)
        ATTN_SCALE = float(np.sqrt(D_HEAD))
        ROPE_BASE = 10000.0

        def _rope_cos_sin(seq_len, d_head, dtype):
            inv_freq = 1.0 / ROPE_BASE ** (jnp.arange(0, d_head, 2, dtype=jnp.float32) / d_head)
            t = jnp.arange(seq_len, dtype=jnp.float32)
            freqs = t[:, None] * inv_freq[None, :]
            return (jnp.cos(freqs).astype(dtype), jnp.sin(freqs).astype(dtype))

        def _apply_rotary(x, cos, sin):
            B, S, H, D = x.shape
            x2 = x.reshape(B, S, H, D // 2, 2)
            xr, xi = (x2[..., 0], x2[..., 1])
            c = cos[None, :, None, :]
            s = sin[None, :, None, :]
            outr = xr * c - xi * s
            outi = xr * s + xi * c
            return jnp.stack([outr, outi], axis=-1).reshape(B, S, H, D)
        B, S, _ = resid_pre.shape
        q = jnp.einsum('bpd,hde->bphe', resid_pre, W_Q) + b_Q
        k = jnp.einsum('bpd,hde->bphe', resid_pre, W_K) + b_K
        v = jnp.einsum('bpd,hde->bphe', resid_pre, W_V) + b_V
        cos, sin = _rope_cos_sin(S, D_HEAD, q.dtype)
        q = _apply_rotary(q, cos, sin)
        k = _apply_rotary(k, cos, sin)
        scores = jnp.einsum('bqhd,bkhd->bhqk', q, k) / ATTN_SCALE
        causal = jnp.tril(jnp.ones((S, S), dtype=bool))
        scores = jnp.where(causal[None, None], scores, jnp.zeros((), dtype=scores.dtype))
        max_v = jnp.max(jnp.abs(scores), axis=-1, keepdims=True)
        sgn = jnp.sign(scores)
        attn_w = sgn * jnp.exp(sgn * scores - max_v)
        attn = attn_w / (jnp.sum(jnp.abs(attn_w), axis=-1, keepdims=True) + 1e-06)
        z = jnp.einsum('bkhd,bhqk->bqhd', v, attn)
        out = jnp.einsum('bqhd,hdm->bqm', z, W_O) + b_O
        return out

    def _L0_ffn_ref(hidden_states, wg, w1, v1, w2):
        import jax, jax.numpy as jnp
        import numpy as np
        E = 32
        K = 8
        H = 512
        F = 192
        B, S = (1, 256)

        def _moe(x, wg, w1, v1, w2):
            T = x.shape[0]
            logits = x @ wg.T
            scores = jax.nn.softmax(logits, axis=-1)
            weights, idx = jax.lax.top_k(scores, K)
            weights = weights / jnp.sum(weights, axis=-1, keepdims=True)
            flat_e = idx.reshape(-1)
            flat_t = jnp.repeat(jnp.arange(T), K)
            flat_w = weights.reshape(-1)
            order = jnp.argsort(flat_e)
            e_s = flat_e[order]
            t_s = flat_t[order]
            w_s = flat_w[order]
            group_sizes = jnp.bincount(e_s, length=E).astype(jnp.int32)
            xs = x[t_s]
            g = jax.lax.ragged_dot(xs, w1, group_sizes)
            u = jax.lax.ragged_dot(xs, v1, group_sizes)
            h = jax.nn.silu(g) * u
            ys = jax.lax.ragged_dot(h, w2, group_sizes)
            out = jnp.zeros((T, x.shape[1]), x.dtype).at[t_s].add(ys * w_s[:, None])
            return out
        Bb, Ss, Hh = hidden_states.shape
        x = hidden_states.reshape(Bb * Ss, Hh)
        out = _moe(x, wg, w1, v1, w2)
        return out.reshape(Bb, Ss, Hh)
    h = _L0_tok_ref(x, L0_tok_weight, L0_tok_lora_A, L0_tok_lora_B)
    h = h + _L0_attn_ref(_layernorm(h, axis=-1), L0_attn_W_Q, L0_attn_W_K, L0_attn_W_V, L0_attn_W_O, L0_attn_b_Q, L0_attn_b_K, L0_attn_b_V, L0_attn_b_O)
    h = h + _L0_ffn_ref(_layernorm(h, axis=-1), L0_ffn_wg, L0_ffn_w1, L0_ffn_v1, L0_ffn_w2)
    return h

_drawn_inputs = setup_inputs


def setup_inputs(seed=0):
    import zlib

    import numpy as np

    out = dict(_drawn_inputs(seed))
    spreads = {'L0_attn_b_Q': (0.0, 0.61),
     'L0_attn_b_K': (0.0, 0.478),
     'L0_attn_b_V': (0.0, 0.66),
     'L0_attn_b_O': (0.0, 0.1)}
    factors = {'L0_ffn_wg': 6.174, 'L0_ffn_w1': 5.529, 'L0_ffn_v1': 5.406, 'L0_ffn_w2': 5.404}
    for name, (base, spread) in spreads.items():
        noise = np.random.default_rng([zlib.crc32(name.encode()), seed]).standard_normal(out[name].shape)
        drawn = base * np.exp(spread * noise) if base else spread * noise
        out[name] = jnp.asarray(drawn.astype(out[name].dtype))
    for name, factor in factors.items():
        out[name] = (out[name] * factor).astype(out[name].dtype)
    return out
```

```python
from contextlib import ExitStack

import concourse.bass as bass
from concourse import mybir

P = 128
F32 = mybir.dt.float32
F16 = mybir.dt.float16
BF16 = mybir.dt.bfloat16
U32 = mybir.dt.uint32
I32 = mybir.dt.int32
ALU = mybir.AluOpType
ACT = mybir.ActivationFunctionType
AX = mybir.AxisListType

T = 2048
NT = T // P
D = 512
DC = D // P
H = 16
R = 64
LORA_SCALE = 128.0 / 8.0
EPS = 1e-5
E = 32
TOPK = 8
F = 192
NB = T // 512

WS = 64.0
PS = 256.0
ZS = 64.0
QS = 8.0
SCORE = 1.0 / (QS * QS * float(P) ** 0.5)


def wait(eng, sem, n):
    if isinstance(n, int) and n <= 0:
        return
    eng.wait_ge(sem, n)


def chunks(i):
    w = P * (i + 1)
    return [(0, w)] if w <= 1024 else [(0, 1024), (1024, w - 1024)]


def banks(i):
    return [(b, min(4, i + 1 - b)) for b in range(0, i + 1, 4)]


GROUPS = [0, 3, 1, 2]
TILES = [4 * g + j for g in GROUPS for j in range(4)]


def chunk_no(p):
    return sum(len(chunks(i)) for i in TILES[:p])


def bank_no(p):
    return sum(len(banks(i)) for i in TILES[:p])


NCH = chunk_no(NT)
NBK = bank_no(NT)
NPB = 3 * NB


def embed_phase(nc, d, x_hi, x_lo):
    with ExitStack() as ctx:
        sb = lambda name, shape, dt=F32: ctx.enter_context(nc.sbuf_tensor(name, shape, dt))
        ps = lambda name, shape: ctx.enter_context(nc.psum_tensor(name, shape, F32))
        sem = lambda name: ctx.enter_context(nc.semaphore(name))
        RING = 4
        idx = sb("idx", [P, NT], I32)
        ident = sb("ident_a", [P, P])
        lora_b = sb("lora_b", [R, D])
        power = sb("power_a", [P, 1])
        base = [sb(f"base{i}", [P, D]) for i in range(RING)]
        rows = [sb(f"rows{i}", [P, R]) for i in range(RING)]
        rows_t = [sb(f"rows_t{i}", [R, P]) for i in range(2)]
        hid = [sb(f"hid{i}", [P, D]) for i in range(2)]
        norm = [sb(f"norm{i}", [P, D]) for i in range(2)]
        stats = [sb(f"stats{i}", [P, 6]) for i in range(2)]
        mv = [sb(f"mv{i}", [P, 2]) for i in range(2)]
        rstd = [sb(f"rstd{i}", [P, 1]) for i in range(2)]
        p_rows = [ps(f"p_rows{i}", [P, 512]) for i in range(2)]
        p_lora = [ps(f"p_lora{i}", [P, 512]) for i in range(2)]
        p_norm = [ps(f"p_norm{i}", [P, 512]) for i in range(2)]
        consts_in = sem("a_consts_in")
        idx_in = sem("a_idx_in")
        power_set = sem("a_power_set")
        base_in = [sem(f"a_base_in{i}") for i in range(RING)]
        rows_in = [sem(f"a_rows_in{i}") for i in range(RING)]
        rows_turned = sem("a_rows_turned")
        rows_copied = sem("a_rows_copied")
        lora_done = sem("a_lora_done")
        hid_done = sem("a_hid_done")
        hid_out = [sem(f"a_hid_out{i}") for i in range(2)]
        stats_done = sem("a_stats_done")
        mv_done = sem("a_mv_done")
        var_eps = sem("a_var_eps")
        rstd_done = sem("a_rstd_done")
        norm_done = sem("a_norm_done")
        norm_turned = sem("a_norm_turned")
        hi_done = sem("a_hi_done")
        lo_done = sem("a_lo_done")
        block = ctx.enter_context(nc.Block())

        @block.sync
        def _(sp):
            sp.dma_start(idx[:, :], d["idx"]).then_inc(idx_in, 16)
            sp.dma_start(ident[:, :], d["ident"]).then_inc(consts_in, 16)
            sp.dma_start(lora_b[:, :], d["lora_b"]).then_inc(consts_in, 16)
            for t in range(NT):
                sp.wait_ge(hid_done, t + 1)
                sp.dma_start(d["h"][t * P:(t + 1) * P, :], hid[t % 2][:, :]).then_inc(hid_out[t % 2], 16)
            for i in range(2):
                sp.wait_ge(hid_out[i], 16 * NT // 2)

        @block.gpsimd
        def _(pool):
            pool.memset(power[:, :], -0.5).then_inc(power_set, 1)
            pool.wait_ge(idx_in, 16)
            pool.wait_ge(power_set, 1)

            def gather(t):
                s = t % RING
                wait(pool, hid_done, t - RING + 1)
                off = bass.IndirectOffsetOnAxis(ap=idx[:, t:t + 1].bitcast(U32), axis=0)
                pool.indirect_dma_start(base[s][:, :], None, d["emb"], off).then_inc(base_in[s], 16)
                off = bass.IndirectOffsetOnAxis(ap=idx[:, t:t + 1].bitcast(U32), axis=0)
                pool.indirect_dma_start(rows[s][:, :], None, d["lora_at"], off).then_inc(rows_in[s], 16)

            for t in range(RING - 1):
                gather(t)
            for t in range(NT):
                if t + RING - 1 < NT:
                    gather(t + RING - 1)
                pool.wait_ge(var_eps, t + 1)
                wait(pool, norm_done, t - 1)
                pool.tensor_tensor(rstd[t % 2][:, :], mv[t % 2][:, 1:2], power[:, :], ALU.pow).then_inc(rstd_done, 1)

        @block.tensor
        def _(pe):
            pe.wait_ge(consts_in, 32)

            def turn_rows(t):
                pe.wait_ge(rows_in[t % RING], 16 * (t // RING + 1))
                wait(pe, rows_copied, t - 1)
                pe.transpose(p_rows[t % 2][0:R, 0:P], rows[t % RING][:, :], ident[:, :]).then_inc(rows_turned, 1)

            turn_rows(0)
            for t in range(NT):
                if t + 1 < NT:
                    turn_rows(t + 1)
                pe.wait_ge(rows_copied, t + 1)
                wait(pe, hid_done, t - 1)
                pe.matmul(p_lora[t % 2][:, :], rows_t[t % 2][:, :], lora_b[:, :], start=True,
                          stop=True).then_inc(lora_done, 1)
                pe.wait_ge(norm_done, t + 1)
                wait(pe, lo_done, t - 1)
                for c in range(DC):
                    last = pe.transpose(p_norm[t % 2][:, c * P:(c + 1) * P], norm[t % 2][:, c * P:(c + 1) * P],
                                        ident[:, :])
                last.then_inc(norm_turned, 1)

        @block.vector
        def _(v):
            for t in range(NT):
                s = t % 2
                v.wait_ge(rows_turned, t + 1)
                wait(v, lora_done, t - 1)
                v.tensor_copy(rows_t[s][:, :], p_rows[s][0:R, 0:P]).then_inc(rows_copied, 1)
                v.wait_ge(lora_done, t + 1)
                v.wait_ge(base_in[t % RING], 16 * (t // RING + 1))
                wait(v, hid_out[s], 16 * (t // 2))
                v.scalar_tensor_tensor(hid[s][:, :], p_lora[s][:, :], LORA_SCALE, base[t % RING][:, :], ALU.mult,
                                       ALU.add).then_inc(hid_done, 1)
                v.wait_ge(hid_done, t + 1)
                v.bn_stats(stats[s][:, :], hid[s][:, :]).then_inc(stats_done, 1)
                v.wait_ge(stats_done, t + 1)
                v.bn_aggr(mv[s][:, :], stats[s][:, :]).then_inc(mv_done, 1)
                v.wait_ge(mv_done, t + 1)
                v.tensor_scalar(mv[s][:, 1:2], mv[s][:, 1:2], EPS, None, ALU.add).then_inc(var_eps, 1)
                v.wait_ge(rstd_done, t + 1)
                v.tensor_scalar(norm[s][:, :], hid[s][:, :], mv[s][:, 0:1], rstd[s][:, 0:1], ALU.subtract,
                                ALU.mult).then_inc(norm_done, 1)
                v.wait_ge(hi_done, t + 1)
                cols = slice(t * P, (t + 1) * P)
                v.tensor_tensor(x_lo[:, :, cols], p_norm[s][:, :].rearrange("p (c n) -> p c n", c=DC),
                                x_hi[:, :, cols], ALU.subtract).then_inc(lo_done, 1)

        @block.scalar
        def _(act):
            for t in range(NT):
                act.wait_ge(norm_turned, t + 1)
                act.activation(x_hi[:, :, t * P:(t + 1) * P], p_norm[t % 2][:, :].rearrange("p (c n) -> p c n", c=DC),
                               ACT.Copy).then_inc(hi_done, 1)


def attention_phase(nc, d, x_hi, x_lo):
    with ExitStack() as ctx:
        sb = lambda name, shape, dt=F32: ctx.enter_context(nc.sbuf_tensor(name, shape, dt))
        ps = lambda name, shape: ctx.enter_context(nc.psum_tensor(name, shape, F32))
        sem = lambda name: ctx.enter_context(nc.semaphore(name))
        ident = sb("ident_b", [P, P])
        mask = sb("mask", [P, P])
        mask16 = sb("mask16", [P, P], BF16)
        ones = sb("ones", [P, P])
        cos = sb("cos", [P, T])
        sin = sb("sin", [P, T])
        bqk = sb("bqk", [P, 2, H])
        w_in = sb("w_in", [P, 3, DC, P])
        w_hi = sb("w_hi", [P, 3, DC, P], F16)
        w_lo = sb("w_lo", [P, 3, DC, P], F16)
        bv = [sb(f"bv{i}", [P, P]) for i in range(2)]
        by_cos = [sb(f"by_cos{i}", [P, 512]) for i in range(2)]
        by_sin = [sb(f"by_sin{i}", [P, 512]) for i in range(2)]
        turned = [sb(f"turned{i}", [P, 512]) for i in range(2)]
        q_hi = [sb(f"q_hi{i}", [P, T], F16) for i in range(2)]
        q_lo = [sb(f"q_lo{i}", [P, T], F16) for i in range(2)]
        k_hi = [sb(f"k_hi{i}", [P, T], F16) for i in range(2)]
        k_lo = [sb(f"k_lo{i}", [P, T], F16) for i in range(2)]
        v_hi = [sb(f"v_hi{i}", [P, NT, P], F16) for i in range(2)]
        v_lo = [sb(f"v_lo{i}", [P, NT, P], F16) for i in range(2)]
        a = [sb(f"a{i}", [P, P * (13 + i)]) for i in range(4)]
        sign = [sb(f"sign{i}", [P, P * (13 + i)], BF16) for i in range(4)]
        bias = sb("bias", [P, 4])
        total = sb("total", [P, 4])
        total_eps = sb("total_eps", [P, 4])
        inv_total = sb("inv_total", [P, 4])
        diag = sb("diag", [P, 4, P])
        inv_row = sb("inv_row", [P, 512])
        wt_hi = sb("wt_hi", [P, NT, 512], F16)
        wt_lo = sb("wt_lo", [P, NT, 512], F16)
        z = sb("z", [P, 512])
        z_half = sb("z_half", [P, 2, 512], F16)
        p_score = [ps(f"p_score{i}", [P, 1024]) for i in range(2)]
        p_turn = [ps(f"p_turn{i}", [P, 512]) for i in range(2)]
        p_proj = ps("p_proj", [P, 512])
        p_z = ps("p_z", [P, 512])

        consts_in = sem("b_consts_in")
        consts_set = sem("b_consts_set")
        mask_done = sem("mask_done")
        w_loaded = sem("w_loaded")
        bias_scaled = sem("bias_scaled")
        w_hi_done = sem("w_hi_done")
        w_lo_done = sem("w_lo_done")
        proj_done = sem("proj_done")
        cos_done = sem("cos_done")
        proj_read = sem("proj_read")
        turned_done = sem("turned_done")
        proj_hi_done = sem("proj_hi_done")
        proj_split = sem("proj_split")
        scores_done = sem("scores_done")
        masked = sem("masked")
        sign_masked = sem("sign_masked")
        bias_done = sem("bias_done")
        abs_done = sem("abs_done")
        sign_done = sem("sign_done")
        exp_done = sem("exp_done")
        signed_done = sem("signed_done")
        total_done = sem("total_done")
        eps_added = sem("eps_added")
        inv_done = sem("inv_done")
        diag_done = sem("diag_done")
        inv_row_done = sem("inv_row_done")
        inv_row_copied = sem("inv_row_copied")
        wt_turned = sem("wt_turned")
        wt_hi_done = sem("wt_hi_done")
        wt_split = sem("wt_split")
        pv_done = sem("pv_done")
        z_read = sem("z_read")
        z_hi_done = sem("z_hi_done")
        z_split = sem("z_split")
        z_out = sem("z_out")
        block = ctx.enter_context(nc.Block())

        LAG = 3
        FILL = 3
        WARM = H // 2 - 1

        def heads(eng, step):
            for i in range(NT):
                step(0, 0, i, None)
            with eng.Fori(0, WARM) as pair:
                for u in range(2):
                    for i in range(NT):
                        step(pair * 2 + (1 + u), (1 + u) % 2, i, True)
            for i in range(NT + LAG + 2):
                step(H - 1, (H - 1) % 2, i, False)

        def lagged(h, i, by, prev):
            if i - by >= NT:
                return None
            if i - by >= 0:
                return h, 0, i - by
            return None if prev is None else (h - 1, 1, i - by + NT)

        def group_at(h, i, phase, prev):
            g, rest = divmod(i - 3 - phase, 4)
            if rest or g > 3:
                return None
            if g >= 0:
                return h, 0, g
            return None if prev is None else (h - 1, 1, g + 4)

        def filler_at(i, by, prev):
            k = i - FILL - by
            return k if prev is not False and 0 <= k < NPB else None

        @block.sync
        def _(sp):
            for dst, name in ((ident, "ident"), (mask, "mask"), (cos, "cos"), (sin, "sin"), (bqk, "bqk")):
                sp.dma_start(dst[:, :] if len(dst.shape) == 2 else dst[:, :, :], d[name]).then_inc(consts_in, 16)

            def load(n, parity):
                wait(sp, w_lo_done, n)
                sp.dma_start(w_in[:, :, :, :], d["wqkv"][n] if isinstance(n, int) else
                             d["wqkv"][bass.ds(n, 1)].rearrange("a p m c e -> (a p) m c e")).then_inc(w_loaded, 16)
                sp.dma_start(bv[parity][:, :], (d["bv"][n:n + 1, :] if isinstance(n, int) else
                             d["bv"][bass.ds(n, 1), :]).to_broadcast([P, P])).then_inc(w_loaded, 16)

            load(0, 0)
            load(1, 1)

            def step(h, parity, i, prev):
                if i == 2 and prev is not False:
                    load(h + 2, parity)
                got = group_at(h, i, LAG + 2, prev)
                if got:
                    gh, _, g = got
                    sp.wait_ge(z_split, 4 * gh + g + 1)
                    rows = slice(2 * gh, 2 * gh + 2) if isinstance(gh, int) else bass.ds(gh * 2, 2)
                    cols = slice(GROUPS[g] * 512, (GROUPS[g] + 1) * 512)
                    sp.dma_start(d["z"][:, rows, cols], z_half[:, :, :]).then_inc(z_out, 16)

            heads(sp, step)
            sp.wait_ge(z_out, 16 * 4 * H)

        @block.tensor
        def _(pe):
            pe.wait_ge(consts_in, 80)
            pe.wait_ge(consts_set, 1)

            def project(h, parity, k, quarters):
                b, what = k // 3, k % 3
                if 0 in quarters:
                    if k == 0:
                        pe.wait_ge(w_lo_done, h + 1)
                    wait(pe, proj_read, NPB * h + k)
                for r in quarters:
                    if what < 2:
                        for n, (wx, xx) in enumerate(((w_hi, x_hi), (w_lo, x_hi), (w_hi, x_lo))):
                            last = pe.matmul(p_proj[:, :], wx[:, what, r, :], xx[:, r, b * 512:(b + 1) * 512],
                                             start=(r == 0 and n == 0), stop=(r == DC - 1 and n == 2))
                        continue
                    cols = slice(b * 512 + r * P, b * 512 + (r + 1) * P)
                    for c in range(DC):
                        for n, (wx, xx) in enumerate(((w_hi, x_hi), (w_lo, x_hi), (w_hi, x_lo))):
                            last = pe.matmul(p_proj[:, r * P:(r + 1) * P], xx[:, c, cols], wx[:, what, c, :],
                                             start=(c == 0 and n == 0), stop=(c == DC - 1 and n == 2))
                if 3 in quarters:
                    last.then_inc(proj_done, 1)

            def scores(h, parity, p, quarter):
                i = TILES[p]
                if i % 4 == 0 and quarter == 0:
                    pe.wait_ge(proj_split, NPB * h + 3 * (i // 4) + 2)
                c0 = 512 * quarter
                m = min(512, P * (i + 1) - c0)
                if m <= 0:
                    return
                n = quarter // 2
                no = NCH * h + chunk_no(p) + n
                s = (chunk_no(p) + n) % 2
                if quarter % 2 == 0:
                    wait(pe, sign_done, no - 1)
                o = c0 % 1024
                for x, (qx, kx) in enumerate(((q_hi, k_hi), (q_hi, k_lo), (q_lo, k_hi))):
                    last = pe.matmul(p_score[s][:, o:o + m], qx[parity][:, i * P:(i + 1) * P],
                                     kx[parity][:, c0:c0 + m], start=(x == 0), stop=(x == 2))
                if o + m == chunks(i)[n][1]:
                    last.then_inc(scores_done, 1)

            def turn(h, p, n):
                i = TILES[p]
                if n >= len(banks(i)):
                    return
                b, m = banks(i)[n]
                no = NBK * h + bank_no(p) + n
                s = (bank_no(p) + n) % 2
                pe.wait_ge(signed_done, no + 1)
                wait(pe, wt_split, no - 1)
                for j in range(m):
                    last = pe.transpose(p_turn[s][:, j * P:(j + 1) * P], a[i % 4][:, (b + j) * P:(b + j + 1) * P],
                                        ident[:, :])
                last.then_inc(wt_turned, 1)

            def row_of_inverses(h, g):
                pe.wait_ge(diag_done, 4 * h + g + 1)
                wait(pe, z_read, 4 * h + g)
                pe.matmul(p_z[:, :], ones[:, :], diag[:, :, :].rearrange("p j n -> p (j n)"), start=True,
                          stop=True).then_inc(inv_row_done, 1)

            def values(h, parity, q, quarter):
                g = GROUPS[q]
                if quarter > g:
                    return
                if quarter == 0:
                    pe.wait_ge(inv_row_copied, 4 * h + q + 1)
                    pe.wait_ge(proj_split, NPB * h + 3 * g + 3)
                    pe.wait_ge(wt_split, NBK * h + bank_no(4 * q + 4))
                for b in range(4 * quarter, 4 * quarter + 4):
                    o = max(0, b - 4 * g) * P
                    for p, (vx, wx) in enumerate(((v_hi, wt_hi), (v_hi, wt_lo), (v_lo, wt_hi))):
                        last = pe.matmul(p_z[:, o:], vx[parity][:, b, :], wx[:, b, o:], start=(b == 0 and p == 0),
                                         stop=(b == 4 * g + 3 and p == 2))
                if quarter == g:
                    last.then_inc(pv_done, 1)

            for k in range(NPB):
                project(0, 0, k, range(4))

            def step(h, parity, i, prev):
                for n in range(4):
                    if i < NT:
                        scores(h, parity, i, n)
                    if got := group_at(h, i, LAG + 1, prev):
                        values(got[0], (parity + got[1]) % 2, got[2], n)
                    if got := lagged(h, i, LAG, prev):
                        turn(got[0], got[2], n)
                    k = filler_at(i, 0, prev)
                    if k is not None and n >= 2:
                        project(h + 1, 1 - parity, k, (2 * n - 4, 2 * n - 3))
                if got := group_at(h, i, LAG, prev):
                    row_of_inverses(got[0], got[2])

            heads(pe, step)

        @block.vector
        def _(v):
            v.memset(ones[:, :], 1.0).then_inc(consts_set, 1)
            v.wait_ge(consts_in, 80)
            v.tensor_scalar(bqk[:, :, :], bqk[:, :, :], WS, None, ALU.mult).then_inc(bias_scaled, 1)
            v.wait_ge(bias_scaled, 1)
            v.wait_ge(consts_set, 1)

            def w_low(n):
                v.wait_ge(w_hi_done, n + 1)
                v.scalar_tensor_tensor(w_lo[:, :, :, :].rearrange("p m c e -> p (m c e)"),
                                       w_in[:, :, :, :].rearrange("p m c e -> p (m c e)"), WS,
                                       w_hi[:, :, :, :].rearrange("p m c e -> p (m c e)"), ALU.mult,
                                       ALU.subtract).then_inc(w_lo_done, 1)

            def read_projection(h, parity, k):
                no = NPB * h + k
                b, what = k // 3, k % 3
                v.wait_ge(proj_done, no + 1)
                wait(v, proj_split, no - 1)
                if what == 2:
                    v.scalar_tensor_tensor(
                        by_cos[k % 2][:, :].rearrange("p (t e) -> p t e", t=4), p_proj[:, :].rearrange("p (t e) -> p t e", t=4),
                        1.0 / WS, bv[parity][:, :].rearrange("p (a e) -> p a e", a=1).to_broadcast([P, 4, P]), ALU.mult,
                        ALU.add).then_inc(proj_read, 1)
                    return
                cols = slice(b * 512, (b + 1) * 512)
                v.scalar_tensor_tensor(by_cos[k % 2][:, :], p_proj[:, :], bqk_at(0, P, what, h), cos[:, cols], ALU.add,
                                       ALU.mult).then_inc(cos_done, 1)
                v.scalar_tensor_tensor(by_sin[k % 2][0:64, :], p_proj[64:P, :], bqk_at(64, P, what, h), sin[0:64, cols],
                                       ALU.add, ALU.mult).then_inc(cos_done, 1)
                v.scalar_tensor_tensor(by_sin[k % 2][64:P, :], p_proj[0:64, :], bqk_at(0, 64, what, h), sin[64:P, cols],
                                       ALU.add, ALU.mult).then_inc(proj_read, 1)

            def bqk_at(p0, p1, what, h):
                if isinstance(h, int):
                    return bqk[p0:p1, what, h:h + 1]
                return bqk[p0:p1, what, bass.ds(h, 1)]

            def maximum(h, p):
                i = TILES[p]
                v.wait_ge(abs_done, NCH * h + chunk_no(p + 1))
                tri = a[i % 4][:, P * i:P * (i + 1)]
                v.tensor_tensor(tri, tri, mask[:, :], ALU.mult).then_inc(masked, 1)
                v.wait_ge(masked, NT * h + p + 1)
                v.tensor_reduce(bias[:, i % 4:i % 4 + 1], a[i % 4][:, 0:P * (i + 1)], AX.X, ALU.max,
                                negate=True).then_inc(bias_done, 1)

            def sum_up(h, p):
                i = TILES[p]
                v.wait_ge(signed_done, NBK * h + bank_no(p + 1))
                v.tensor_reduce(total[:, i % 4:i % 4 + 1], a[i % 4][:, 0:P * (i + 1)], AX.X, ALU.add,
                                apply_absolute_value=True).then_inc(total_done, 1)

            def inverses(h, g):
                m = 4 * h + g
                v.wait_ge(total_done, NT * h + 4 * g + 4)
                v.tensor_scalar(total_eps[:, :], total[:, :], 1e-6, None, ALU.add).then_inc(eps_added, 1)
                v.wait_ge(eps_added, m + 1)
                v.reciprocal(inv_total[:, :], total_eps[:, :]).then_inc(inv_done, 1)
                v.wait_ge(inv_done, m + 1)
                wait(v, inv_row_done, m)
                v.scalar_tensor_tensor(diag[:, :, :],
                                       ident[:, :].rearrange("p (a n) -> p a n", a=1).to_broadcast([P, 4, P]), ZS / PS,
                                       inv_total[:, :].rearrange("p (j a) -> p j a", a=1).to_broadcast([P, 4, P]),
                                       ALU.mult, ALU.mult).then_inc(diag_done, 1)

            def low_halves(h, p, which):
                i = TILES[p]
                for n in which:
                    if n >= len(banks(i)):
                        return
                    b, m = banks(i)[n]
                    no = NBK * h + bank_no(p) + n
                    v.wait_ge(wt_hi_done, no + 1)
                    cols = slice(i % 4 * P, (i % 4 + 1) * P)
                    v.scalar_tensor_tensor(
                        wt_lo[:, b:b + m, cols], p_turn[(bank_no(p) + n) % 2][:, 0:m * P].rearrange("p (j n) -> p j n", j=m),
                        PS, wt_hi[:, b:b + m, cols], ALU.mult, ALU.subtract).then_inc(wt_split, 1)

            def read_z(h, g):
                m = 4 * h + g
                v.wait_ge(pv_done, m + 1)
                wait(v, z_split, m)
                v.tensor_tensor(z[:, :], p_z[:, :], inv_row[:, :], ALU.mult).then_inc(z_read, 1)

            w_low(0)
            for k in range(NPB):
                read_projection(0, 0, k)
            w_low(1)

            def step(h, parity, i, prev):
                k = filler_at(i, 1, prev)
                if k is not None:
                    read_projection(h + 1, 1 - parity, k)
                behind = lagged(h, i, LAG, prev)
                if behind:
                    low_halves(behind[0], behind[2], (0, 1))
                if got := lagged(h, i, 2, prev):
                    sum_up(got[0], got[2])
                if got := group_at(h, i, 2, prev):
                    inverses(got[0], got[2])
                if behind:
                    low_halves(behind[0], behind[2], (2, 3))
                if got := group_at(h, i, LAG + 2, prev):
                    read_z(got[0], got[2])
                if i < NT:
                    maximum(h, i)
                if i == NT - 1 and prev is not False:
                    w_low(h + 2)

            heads(v, step)

        @block.scalar
        def _(act):
            def w_high(n):
                act.wait_ge(w_loaded, 32 * n + 32)
                wait(act, proj_done, NPB * n)
                act.activation(w_hi[:, :, :, :], w_in[:, :, :, :], ACT.Copy, scale=WS).then_inc(w_hi_done, 1)

            def proj_high(h, parity, k):
                no = NPB * h + k
                b, what = k // 3, k % 3
                if what == 2:
                    act.wait_ge(proj_read, no + 1)
                    act.activation(v_hi[parity][:, 4 * b:4 * b + 4, :], by_cos[k % 2][:, :].rearrange("p (t e) -> p t e", t=4),
                                   ACT.Copy).then_inc(proj_hi_done, 1)
                else:
                    act.wait_ge(turned_done, 2 * NB * h + 2 * b + what + 1)
                    act.activation((q_hi, k_hi)[what][parity][:, b * 512:(b + 1) * 512], turned[k % 2][:, :],
                                   ACT.Copy).then_inc(proj_hi_done, 1)

            def abs_and_sign(h, p, n):
                i = TILES[p]
                if n >= len(chunks(i)):
                    return
                c0, w = chunks(i)[n]
                no = NCH * h + chunk_no(p) + n
                s = (chunk_no(p) + n) % 2
                if n == 0:
                    wait(act, total_done, NT * h + p - 3)
                act.wait_ge(scores_done, no + 1)
                act.activation(a[i % 4][:, c0:c0 + w], p_score[s][:, 0:w], ACT.Abs, scale=SCORE).then_inc(abs_done, 1)
                act.activation(sign[i % 4][:, c0:c0 + w], p_score[s][:, 0:w], ACT.Sign).then_inc(sign_done, 1)

            def exponentials(h, p):
                i = TILES[p]
                act.wait_ge(bias_done, NT * h + p + 1)
                act.activation(a[i % 4][:, 0:P * (i + 1)], a[i % 4][:, 0:P * (i + 1)], ACT.Exp,
                               bias=bias[:, i % 4:i % 4 + 1]).then_inc(exp_done, 1)

            def high_halves(h, p, which):
                i = TILES[p]
                for n in which:
                    if n >= len(banks(i)):
                        return
                    b, m = banks(i)[n]
                    no = NBK * h + bank_no(p) + n
                    act.wait_ge(wt_turned, no + 1)
                    act.activation(wt_hi[:, b:b + m, i % 4 * P:(i % 4 + 1) * P],
                                   p_turn[(bank_no(p) + n) % 2][:, 0:m * P].rearrange("p (j n) -> p j n", j=m), ACT.Copy,
                                   scale=PS).then_inc(wt_hi_done, 1)

            def copy_inverses(h, g):
                m = 4 * h + g
                act.wait_ge(inv_row_done, m + 1)
                wait(act, z_read, m)
                act.activation(inv_row[:, :], p_z[:, :], ACT.Copy).then_inc(inv_row_copied, 1)

            def z_high(h, g):
                m = 4 * h + g
                act.wait_ge(z_read, m + 1)
                wait(act, z_out, 16 * m)
                act.activation(z_half[:, 0, :], z[:, :], ACT.Copy).then_inc(z_hi_done, 1)

            w_high(0)
            for k in range(NPB):
                proj_high(0, 0, k)
            w_high(1)

            def step(h, parity, i, prev):
                if got := group_at(h, i, LAG + 1, prev):
                    copy_inverses(got[0], got[2])
                if got := lagged(h, i, 1, prev):
                    exponentials(got[0], got[2])
                behind = lagged(h, i, LAG, prev)
                if behind:
                    high_halves(behind[0], behind[2], (0, 1))
                if i < NT:
                    abs_and_sign(h, i, 0)
                k = filler_at(i, 1, prev)
                if k is not None:
                    proj_high(h + 1, 1 - parity, k)
                if behind:
                    high_halves(behind[0], behind[2], (2, 3))
                if i < NT:
                    abs_and_sign(h, i, 1)
                if got := group_at(h, i, LAG + 2, prev):
                    z_high(got[0], got[2])
                if i == NT - 1 and prev is not False:
                    w_high(h + 2)

            heads(act, step)

        @block.gpsimd
        def _(pool):
            pool.wait_ge(consts_in, 80)
            pool.tensor_copy(mask16[:, :], mask[:, :]).then_inc(mask_done, 1)
            pool.wait_ge(mask_done, 1)

            def rotate(h, k):
                no = NPB * h + k
                b, what = k // 3, k % 3
                if what == 2:
                    return
                pool.wait_ge(proj_read, no + 1)
                pool.wait_ge(cos_done, 2 * (2 * NB * h + 2 * b + what + 1))
                pool.tensor_tensor(turned[k % 2][:, :], by_cos[k % 2][:, :], by_sin[k % 2][:, :], ALU.add).then_inc(turned_done, 1)

            def proj_low(h, parity, k):
                no = NPB * h + k
                b, what = k // 3, k % 3
                pool.wait_ge(proj_hi_done, no + 1)
                if what == 2:
                    pool.tensor_tensor(v_lo[parity][:, 4 * b:4 * b + 4, :].rearrange("p t e -> p (t e)"), by_cos[k % 2][:, :],
                                       v_hi[parity][:, 4 * b:4 * b + 4, :].rearrange("p t e -> p (t e)"),
                                       ALU.subtract).then_inc(proj_split, 1)
                else:
                    pool.wait_ge(turned_done, 2 * NB * h + 2 * b + what + 1)
                    cols = slice(b * 512, (b + 1) * 512)
                    pool.tensor_tensor((q_lo, k_lo)[what][parity][:, cols], turned[k % 2][:, :],
                                       (q_hi, k_hi)[what][parity][:, cols], ALU.subtract).then_inc(proj_split, 1)

            def put_sign(h, p):
                i = TILES[p]
                pool.wait_ge(sign_done, NCH * h + chunk_no(p + 1))
                tri = sign[i % 4][:, P * i:P * (i + 1)]
                pool.tensor_tensor(tri, tri, mask16[:, :], ALU.mult).then_inc(sign_masked, 1)
                pool.wait_ge(exp_done, NT * h + p + 1)
                pool.wait_ge(sign_masked, NT * h + p + 1)
                for b, m in banks(i):
                    cols = slice(b * P, (b + m) * P)
                    pool.tensor_tensor(a[i % 4][:, cols], a[i % 4][:, cols], sign[i % 4][:, cols],
                                       ALU.mult).then_inc(signed_done, 1)

            def z_low(h, g):
                pool.wait_ge(z_hi_done, 4 * h + g + 1)
                pool.tensor_tensor(z_half[:, 1, :], z[:, :], z_half[:, 0, :], ALU.subtract).then_inc(z_split, 1)

            for k in range(NPB):
                rotate(0, k)
                proj_low(0, 0, k)

            def step(h, parity, i, prev):
                k = filler_at(i, 1, prev)
                if k is not None:
                    rotate(h + 1, k)
                if got := lagged(h, i, 1, prev):
                    put_sign(got[0], got[2])
                if k is not None:
                    proj_low(h + 1, 1 - parity, k)
                if got := group_at(h, i, LAG + 2, prev):
                    z_low(got[0], got[2])

            heads(pool, step)


def output_phase(nc, d, x_hi, x_lo, acc, gate):
    with ExitStack() as ctx:
        sb = lambda name, shape, dt=F32: ctx.enter_context(nc.sbuf_tensor(name, shape, dt))
        ps = lambda name, shape: ctx.enter_context(nc.psum_tensor(name, shape, F32))
        sem = lambda name: ctx.enter_context(nc.semaphore(name))
        PART = 4
        ident = sb("ident_c", [P, P])
        power = sb("power_c", [P, 1])
        bo = sb("bo", [P, D])
        wg_in = sb("wg_in", [P, DC, E])
        wg_hi = sb("wg_hi", [P, DC, E], F16)
        wg_lo = sb("wg_lo", [P, DC, E], F16)
        wo_in = sb("wo_in", [P, PART, D])
        wo_hi = sb("wo_hi", [P, H, D], F16)
        wo_lo = sb("wo_lo", [P, H, D], F16)
        zs = [sb(f"zs{i}", [P, 2 * H, 512], F16) for i in range(2)]
        hid = [sb(f"hid_c{i}", [P, D]) for i in range(2)]
        norm = [sb(f"norm_c{i}", [P, D]) for i in range(2)]
        xt_hi = [sb(f"xt_hi{i}", [P, DC, P], F16) for i in range(2)]
        xt_lo = [sb(f"xt_lo{i}", [P, DC, P], F16) for i in range(2)]
        stats = sb("stats_c", [P, 6])
        mv = sb("mv_c", [P, 2])
        rstd = sb("rstd_c", [P, 1])
        top_bias = sb("top_bias", [P, 1])
        e_sum = sb("e_sum", [P, 1])
        e_inv = sb("e_inv", [P, 1])
        expd = sb("expd", [P, E])
        probs = sb("probs", [P, E])
        top8 = sb("top8", [P, 8])
        rest = sb("rest", [P, E])
        chosen = sb("chosen", [P, E])
        chosen_sum = sb("chosen_sum", [P, 1])
        chosen_inv = sb("chosen_inv", [P, 1])
        p_out = [ps(f"p_out{i}", [P, 512]) for i in range(2)]
        p_norm = [ps(f"p_norm_c{i}", [P, 512]) for i in range(2)]
        p_logit = ps("p_logit", [P, 512])
        consts_in = sem("c_consts_in")
        power_set = sem("c_power_set")
        wo_loaded = sem("wo_loaded")
        wo_hi_done = sem("wo_hi_done")
        wo_lo_done = sem("wo_lo_done")
        zs_in = [sem(f"zs_in{i}") for i in range(2)]
        hid_in = [sem(f"c_hid_in{i}") for i in range(2)]
        biased = sem("c_biased")
        out_done = sem("out_done")
        acc_done = sem("acc_done")
        kept = sem("kept")
        stats_done = sem("c_stats_done")
        mv_done = sem("c_mv_done")
        var_eps = sem("c_var_eps")
        rstd_done = sem("c_rstd_done")
        norm_done = sem("c_norm_done")
        norm_turned = sem("c_norm_turned")
        hi_done = sem("c_hi_done")
        lo_done = sem("c_lo_done")
        x_kept = sem("x_kept")
        logits_done = sem("logits_done")
        top_bias_done = sem("top_bias_done")
        exp_done = sem("c_exp_done")
        e_inv_done = sem("e_inv_done")
        probs_done = sem("probs_done")
        top8_done = sem("top8_done")
        rest_done = sem("rest_done")
        chosen_done = sem("chosen_done")
        chosen_inv_done = sem("chosen_inv_done")
        gate_done = sem("gate_done")
        block = ctx.enter_context(nc.Block())
        PAIRS = NB // 2

        def tiles(eng, step):
            with eng.Fori(0, PAIRS) as pair:
                for n in range(8):
                    step(pair * 8 + n, n, pair)

        @block.sync
        def _(sp):
            sp.dma_start(ident[:, :], d["ident"]).then_inc(consts_in, 16)
            sp.dma_start(wg_in[:, :, :], d["wg"]).then_inc(consts_in, 16)
            sp.dma_start(bo[:, :], d["bo"].to_broadcast([P, D])).then_inc(consts_in, 16)
            for n in range(H // PART):
                wait(sp, wo_lo_done, n + 1 if n else 0)
                sp.dma_start(wo_in[:, :, :], d["wo"][:, n * PART:(n + 1) * PART, :]).then_inc(wo_loaded, 16)

            def load_z(t, n, pair):
                if n % 4 == 0:
                    sp.wait_ge(out_done, t + 4)
                    sp.dma_start(zs[n // 4][:, :, :], d["z"][:, :, bass.ds(pair * 1024 + n // 4 * 512, 512)]).then_inc(zs_in[n // 4], 16)

            tiles(sp, load_z)

        @block.gpsimd
        def _(pool):
            pool.memset(power[:, :], -0.5).then_inc(power_set, 1)
            pool.sem_inc(kept, 2)
            pool.wait_ge(power_set, 1)
            pool.wait_ge(consts_in, 48)

            def step(t, n, pair):
                s = n % 2
                pool.wait_ge(norm_done, t + 1)
                pool.wait_ge(kept, t + 1)
                pool.dma_start(hid[s][:, :], d["h"][bass.ds(t * P, P), :]).then_inc(hid_in[s], 16)
                pool.wait_ge(hid_in[s], 16 * (pair * 4 + (n // 2 + 1)))
                pool.tensor_tensor(hid[s][:, :], hid[s][:, :], bo[:, :], ALU.add).then_inc(biased, 1)
                pool.wait_ge(var_eps, t + 1)
                pool.tensor_tensor(rstd[:, :], mv[:, 1:2], power[:, :], ALU.pow).then_inc(rstd_done, 1)
                pool.tensor_copy(acc[:, bass.ds(t, 1), :].rearrange("p a n -> p (a n)"), hid[s][:, :]).then_inc(kept, 1)

            tiles(pool, step)

        @block.tensor
        def _(pe):
            pe.sem_inc(out_done, 8)
            pe.wait_ge(consts_in, 48)
            pe.wait_ge(wo_lo_done, H // PART + 1)

            def output(t, n, pair, part):
                if part == 0:
                    if n % 4 == 0:
                        pe.wait_ge(zs_in[n // 4], 16 * (pair + 1))
                    pe.wait_ge(acc_done, t + 1)
                cols = slice(n % 4 * P, (n % 4 + 1) * P)
                for h in range(H // 2 * part, H // 2 * (part + 1)):
                    for p, (half, w) in enumerate(((0, wo_hi), (0, wo_lo), (1, wo_hi))):
                        last = pe.matmul(p_out[n % 2][:, :], zs[n // 4][:, 2 * h + half, cols], w[:, h, :],
                                         start=(h == 0 and p == 0), stop=(h == H - 1 and p == 2))
                if part == 1:
                    last.then_inc(out_done, 1)

            def turn(t, s):
                pe.wait_ge(norm_done, t + 3)
                for c in range(DC):
                    last = pe.transpose(p_norm[s][:, c * P:(c + 1) * P], norm[s][:, c * P:(c + 1) * P], ident[:, :])
                last.then_inc(norm_turned, 1)

            def logits(t, s):
                pe.wait_ge(x_kept, t + 1)
                pe.wait_ge(gate_done, t + 1)
                for c in range(DC):
                    for p, (xx, w) in enumerate(((xt_hi, wg_hi), (xt_hi, wg_lo), (xt_lo, wg_hi), (xt_lo, wg_lo))):
                        last = pe.matmul(p_logit[:, 0:E], xx[s][:, c, :], w[:, c, :], start=(c == 0 and p == 0),
                                         stop=(c == DC - 1 and p == 3))
                last.then_inc(logits_done, 1)

            with pe.Fori(0, PAIRS) as pair:
                for n in range(9):
                    t = pair * 8 + n
                    if n < 8:
                        output(t, n, pair, 0)
                    if n:
                        turn(pair * 8 + (n - 1), (n - 1) % 2)
                    if n < 8:
                        output(t, n, pair, 1)
                    if n:
                        logits(pair * 8 + (n - 1), (n - 1) % 2)

        @block.vector
        def _(v):
            v.wait_ge(consts_in, 48)
            v.wait_ge(wo_hi_done, 1)
            v.scalar_tensor_tensor(wg_lo[:, :, :], wg_in[:, :, :], WS, wg_hi[:, :, :], ALU.mult,
                                   ALU.subtract).then_inc(wo_lo_done, 1)
            for n in range(H // PART):
                v.wait_ge(wo_hi_done, n + 2)
                v.scalar_tensor_tensor(wo_lo[:, n * PART:(n + 1) * PART, :], wo_in[:, :, :], WS,
                                       wo_hi[:, n * PART:(n + 1) * PART, :], ALU.mult, ALU.subtract).then_inc(wo_lo_done, 1)
            v.sem_inc(acc_done, 2)
            v.sem_inc(norm_done, 2)
            v.sem_inc(gate_done, 1)

            def step(t, n, pair):
                s = n % 2
                v.wait_ge(out_done, t + 9)
                v.wait_ge(biased, t + 1)
                row = hid[s][:, :]
                v.scalar_tensor_tensor(row, p_out[s][:, :], 1.0 / (WS * ZS), hid[s][:, :], ALU.mult,
                                       ALU.add).then_inc(acc_done, 1)
                v.wait_ge(consts_in, 48)
                v.wait_ge(acc_done, t + 3)
                v.bn_stats(stats[:, :], row).then_inc(stats_done, 1)
                v.wait_ge(consts_in, 48)
                v.wait_ge(stats_done, t + 1)
                v.bn_aggr(mv[:, :], stats[:, :]).then_inc(mv_done, 1)
                v.wait_ge(mv_done, t + 1)
                v.tensor_scalar(mv[:, 1:2], mv[:, 1:2], EPS, None, ALU.add).then_inc(var_eps, 1)
                v.wait_ge(rstd_done, t + 1)
                v.tensor_scalar(norm[s][:, :], row, mv[:, 0:1], rstd[:, 0:1], ALU.subtract, ALU.mult).then_inc(norm_done, 1)
                v.wait_ge(hi_done, t + 1)
                v.tensor_tensor(xt_lo[s][:, :, :], p_norm[s][:, :].rearrange("p (c n) -> p c n", c=DC), xt_hi[s][:, :, :],
                                ALU.subtract).then_inc(lo_done, 1)
                v.wait_ge(lo_done, t + 1)
                cols = bass.ds(t * P, P)
                v.tensor_copy(x_hi[:, :, cols], xt_hi[s][:, :, :])
                v.tensor_copy(x_lo[:, :, cols], xt_lo[s][:, :, :]).then_inc(x_kept, 1)
                v.wait_ge(logits_done, t + 1)
                v.tensor_reduce(top_bias[:, :], p_logit[:, 0:E], AX.X, ALU.max, negate=True).then_inc(top_bias_done, 1)
                v.wait_ge(top_bias_done, 2 * t + 1)
                v.tensor_scalar(top_bias[:, :], top_bias[:, :], 1.0 / WS, None, ALU.mult).then_inc(top_bias_done, 1)
                v.wait_ge(exp_done, t + 1)
                v.reciprocal(e_inv[:, :], e_sum[:, :]).then_inc(e_inv_done, 1)
                v.wait_ge(e_inv_done, t + 1)
                v.tensor_scalar(probs[:, :], expd[:, :], e_inv[:, 0:1], None, ALU.mult).then_inc(probs_done, 1)
                v.wait_ge(consts_in, 48)
                v.wait_ge(probs_done, t + 1)
                v.max(top8[:, :], probs[:, :]).then_inc(top8_done, 1)
                v.wait_ge(consts_in, 48)
                v.wait_ge(top8_done, t + 1)
                v.match_replace(out=rest[:, :], in_to_replace=top8[:, :], in_values=probs[:, :],
                                imm_value=-1.0).then_inc(rest_done, 1)
                v.wait_ge(rest_done, t + 1)
                v.scalar_tensor_tensor(chosen[:, :], rest[:, :], 0.0, probs[:, :], ALU.max, ALU.subtract,
                                       accum_out=chosen_sum[:, :]).then_inc(chosen_done, 1)
                v.wait_ge(chosen_done, t + 1)
                v.reciprocal(chosen_inv[:, :], chosen_sum[:, :]).then_inc(chosen_inv_done, 1)
                v.wait_ge(chosen_inv_done, t + 1)
                v.tensor_scalar(gate[:, bass.ds(t, 1), :].rearrange("p a e -> p (a e)"), chosen[:, :], chosen_inv[:, 0:1],
                                1.0 / WS, ALU.mult, ALU.mult).then_inc(gate_done, 1)

            tiles(v, step)

        @block.scalar
        def _(act):
            act.wait_ge(consts_in, 48)
            act.activation(wg_hi[:, :, :], wg_in[:, :, :], ACT.Copy, scale=WS).then_inc(wo_hi_done, 1)
            for n in range(H // PART):
                act.wait_ge(wo_loaded, 16 * (n + 1))
                act.activation(wo_hi[:, n * PART:(n + 1) * PART, :], wo_in[:, :, :], ACT.Copy, scale=WS).then_inc(wo_hi_done, 1)

            def step(t, n, pair):
                s = n % 2
                act.wait_ge(norm_turned, t + 1)
                act.activation(xt_hi[s][:, :, :], p_norm[s][:, :].rearrange("p (c n) -> p c n", c=DC),
                               ACT.Copy).then_inc(hi_done, 1)
                act.wait_ge(top_bias_done, 2 * t + 2)
                act.activation(expd[:, :], p_logit[:, 0:E], ACT.Exp, bias=top_bias[:, 0:1], scale=1.0 / WS,
                               accum_out=e_sum[:, :]).then_inc(exp_done, 1)

            tiles(act, step)


def expert_phase(nc, d, x_hi, x_lo, acc, gate):
    with ExitStack() as ctx:
        sb = lambda name, shape, dt=F32: ctx.enter_context(nc.sbuf_tensor(name, shape, dt))
        ps = lambda name, shape: ctx.enter_context(nc.psum_tensor(name, shape, F32))
        sem = lambda name: ctx.enter_context(nc.semaphore(name))
        FR = F - P
        AHEAD = NT + 1
        up_in = [sb(f"up_in{i}", [P, DC, 2 * F]) for i in range(2)]
        up_hi = [sb(f"up_hi{i}", [P, DC, 2 * F], F16) for i in range(2)]
        up_lo = [sb(f"up_lo{i}", [P, DC, 2 * F], F16) for i in range(2)]
        down_in = [sb(f"down_in{i}", [P, 2, D]) for i in range(2)]
        down_hi = [sb(f"down_hi{i}", [P, 2, D], F16) for i in range(2)]
        down_lo = [sb(f"down_lo{i}", [P, 2, D], F16) for i in range(2)]
        silu = sb("silu", [P, 2, 512])
        hid = [sb(f"hid_d{i}", [P, 2, 512]) for i in range(2)]
        hid_hi = [sb(f"hid_hi{i}", [P, 2, 512], F16) for i in range(2)]
        hid_lo = [sb(f"hid_lo{i}", [P, 2, 512], F16) for i in range(2)]
        p_up = [ps(f"p_up{i}", [P, 3, 512]) for i in range(2)]
        p_down = [ps(f"p_down{i}", [P, 512]) for i in range(2)]
        up_loaded = [sem(f"up_loaded{i}") for i in range(2)]
        w_hi_done = sem("d_w_hi_done")
        w_lo_done = sem("d_w_lo_done")
        up_done = sem("up_done")
        silu_done = sem("silu_done")
        hid_done = sem("d_hid_done")
        hid_hi_done = sem("hid_hi_done")
        hid_split = sem("hid_split")
        down_done = sem("down_done")
        added = sem("added")
        stored = sem("stored")
        block = ctx.enter_context(nc.Block())

        def experts(eng, body):
            with eng.Fori(0, E // 2) as pair:
                for u in range(2):
                    body(pair * 2 + u, u, pair)

        @block.sync
        def _(sp):
            def load(e, u):
                sp.wait_ge(w_lo_done, e + 1)
                one = lambda a: a[bass.ds(e, 1)]
                sp.dma_start(up_in[u][:, :, :], one(d["up"]).rearrange("a p c f -> (a p) c f")).then_inc(up_loaded[u], 16)
                sp.dma_start(down_in[u][:, 0, :], one(d["down_a"]).rearrange("a p n -> (a p) n")).then_inc(up_loaded[u], 16)
                sp.dma_start(down_in[u][0:FR, 1, :], one(d["down_b"]).rearrange("a p n -> (a p) n")).then_inc(up_loaded[u], 16)

            load(0, 0)
            experts(sp, lambda e, u, pair: load(e + 1, 1 - u))
            sp.wait_ge(added, NT * E + 2)
            sp.dma_start(d["out"].rearrange("(t p) n -> p t n", p=P), acc[:, :, :]).then_inc(stored, 16)
            sp.wait_ge(stored, 16)

        @block.tensor
        def _(pe):
            pe.sem_inc(down_done, AHEAD)

            def up(e, u, b):
                no = NB * e + b
                pe.wait_ge(hid_done, no + 1)
                if b == 0:
                    pe.wait_ge(w_lo_done, e + 3)
                cols = slice(b * 512, (b + 1) * 512)
                for m in range(3):
                    for c in range(DC):
                        for p, (w, xx) in enumerate(((up_hi, x_hi), (up_lo, x_hi), (up_hi, x_lo))):
                            last = pe.matmul(p_up[b % 2][:, m, :], w[u][:, c, m * P:(m + 1) * P], xx[:, c, cols],
                                             start=(c == 0 and p == 0), stop=(c == DC - 1 and p == 2))
                last.then_inc(up_done, 1)

            def down(e, u, b):
                pe.wait_ge(hid_split, NB * e + b + 1)
                for t in range(4):
                    no = NT * e + 4 * b + t
                    pe.wait_ge(added, no + 1)
                    cols = slice(t * P, (t + 1) * P)
                    for k, rows in ((0, P), (1, FR)):
                        for p, (hh, w) in enumerate(((hid_hi, down_hi), (hid_hi, down_lo), (hid_lo, down_hi))):
                            last = pe.matmul(p_down[t % 2][:, :], hh[b % 2][0:rows, k, cols], w[u][0:rows, k, :],
                                             start=(k == 0 and p == 0), stop=(k == 1 and p == 2))
                    last.then_inc(down_done, 1)

            def body(e, u, pair):
                for b in range(NB):
                    up(e, u, b)
                    if b:
                        down(e, u, b - 1)
                down(e, u, NB - 1)

            experts(pe, body)

        @block.scalar
        def _(act):
            def split(e, u, loads):
                act.wait_ge(up_loaded[u], 48 * loads)
                act.wait_ge(down_done, NT * e + 1)
                act.activation(up_hi[u][:, :, :], up_in[u][:, :, :], ACT.Copy, scale=WS)
                act.activation(down_hi[u][:, 0, :], down_in[u][:, 0, :], ACT.Copy, scale=WS)
                act.activation(down_hi[u][0:FR, 1, :], down_in[u][0:FR, 1, :], ACT.Copy, scale=WS).then_inc(w_hi_done, 1)

            def body(e, u, pair):
                for b in range(NB):
                    if b == 1:
                        split(e + 1, 1 - u, pair + (1 + u))
                    act.wait_ge(up_done, NB * e + b + 1)
                    act.wait_ge(hid_done, NB * e + b + 2)
                    act.activation(silu[:, 0, :], p_up[b % 2][:, 0, :], ACT.Silu, scale=1.0 / WS)
                    act.activation(silu[0:FR, 1, :], p_up[b % 2][0:FR, 2, :], ACT.Silu, scale=1.0 / WS).then_inc(silu_done, 1)
                    act.wait_ge(hid_done, NB * e + b + 3)
                    act.activation(hid_hi[b % 2][:, 0, :], hid[b % 2][:, 0, :], ACT.Copy)
                    act.activation(hid_hi[b % 2][0:FR, 1, :], hid[b % 2][0:FR, 1, :], ACT.Copy).then_inc(hid_hi_done, 1)

            split(0, 0, 1)
            experts(act, body)

        @block.vector
        def _(v):
            v.sem_inc(hid_done, 2)
            v.sem_inc(w_lo_done, 2)
            v.sem_inc(added, 2)

            def split(e, u):
                v.wait_ge(w_hi_done, e + 1)
                v.scalar_tensor_tensor(up_lo[u][:, :, :], up_in[u][:, :, :], WS, up_hi[u][:, :, :], ALU.mult, ALU.subtract)
                v.scalar_tensor_tensor(down_lo[u][:, 0, :], down_in[u][:, 0, :], WS, down_hi[u][:, 0, :], ALU.mult,
                                       ALU.subtract)
                v.scalar_tensor_tensor(down_lo[u][0:FR, 1, :], down_in[u][0:FR, 1, :], WS, down_hi[u][0:FR, 1, :],
                                       ALU.mult, ALU.subtract).then_inc(w_lo_done, 1)

            def body(e, u, pair):
                def add(b):
                    for t in range(4):
                        v.wait_ge(down_done, NT * e + (4 * b + t + 1 + AHEAD))
                        tile = 4 * b + t
                        v.scalar_tensor_tensor(acc[:, tile, :], p_down[t % 2][:, :], gate[:, tile, bass.ds(e, 1)],
                                               acc[:, tile, :], ALU.mult, ALU.add).then_inc(added, 1)

                for b in range(NB):
                    if b == 1:
                        split(e + 1, 1 - u)
                    v.wait_ge(silu_done, NB * e + b + 1)
                    v.scalar_tensor_tensor(hid[b % 2][:, 0, :], p_up[b % 2][:, 1, :], 1.0 / WS, silu[:, 0, :], ALU.mult, ALU.mult)
                    v.scalar_tensor_tensor(hid[b % 2][0:FR, 1, :], p_up[b % 2][FR:P, 2, :], 1.0 / WS, silu[0:FR, 1, :],
                                           ALU.mult, ALU.mult).then_inc(hid_done, 1)
                    if b:
                        add(b - 1)
                add(NB - 1)

            split(0, 0)
            experts(v, body)

        @block.gpsimd
        def _(pool):
            def body(e, u, pair):
                for b in range(NB):
                    pool.wait_ge(hid_hi_done, NB * e + b + 1)
                    pool.tensor_tensor(hid_lo[b % 2][:, 0, :], hid[b % 2][:, 0, :], hid_hi[b % 2][:, 0, :], ALU.subtract)
                    pool.tensor_tensor(hid_lo[b % 2][0:FR, 1, :], hid[b % 2][0:FR, 1, :], hid_hi[b % 2][0:FR, 1, :],
                                       ALU.subtract).then_inc(hid_split, 1)

            experts(pool, body)


def build(nc, d):
    with ExitStack() as ctx:
        x_hi = ctx.enter_context(nc.sbuf_tensor("x_hi", [P, DC, T], F16))
        x_lo = ctx.enter_context(nc.sbuf_tensor("x_lo", [P, DC, T], F16))
        embed_phase(nc, d, x_hi, x_lo)
        attention_phase(nc, d, x_hi, x_lo)
        acc = ctx.enter_context(nc.sbuf_tensor("acc", [P, NT, D], F32))
        gate = ctx.enter_context(nc.sbuf_tensor("gate", [P, NT, E], F32))
        output_phase(nc, d, x_hi, x_lo, acc, gate)
        expert_phase(nc, d, x_hi, x_lo, acc, gate)


def host_layout(x, emb, lora_A, lora_B, wq, wk, wv, wo, bq, bk, bv, bo, wg, w1, v1, w2):
    import numpy as np
    turn = np.concatenate([np.arange(0, P, 2), np.arange(1, P, 2)])
    chunked = lambda w: w.reshape(H, DC, P, P).transpose(0, 2, 1, 3)
    wqkv = np.stack([chunked(wq[:, :, turn]), chunked(wk[:, :, turn]), chunked(wv)], axis=2)
    inv_freq = np.float32(1.0) / (10000.0 ** (np.arange(0, P, 2) / P)).astype(np.float32)
    freqs = np.arange(T, dtype=np.float32)[None, :] * inv_freq[:, None]
    cos, sin = np.cos(freqs).astype(np.float32), np.sin(freqs).astype(np.float32)
    gain = np.float32(QS / WS)
    padded = lambda w: np.ascontiguousarray(np.concatenate([w, w[:1]]))
    return {
        "idx": np.ascontiguousarray(x.reshape(NT, P).T),
        "emb": emb,
        "lora_at": np.ascontiguousarray(lora_A.T),
        "lora_b": np.ascontiguousarray(lora_B.T),
        "ident": np.eye(P, dtype=np.float32),
        "mask": np.tril(np.ones((P, P), np.float32)),
        "cos": np.concatenate([cos, cos]) * gain,
        "sin": np.concatenate([-sin, sin]) * gain,
        "bqk": np.ascontiguousarray(np.stack([bq[:, turn].T, bk[:, turn].T], axis=1)),
        "wqkv": padded(wqkv),
        "bv": padded(bv),
        "wo": np.ascontiguousarray(wo.transpose(1, 0, 2)),
        "bo": bo.reshape(1, D),
        "wg": np.ascontiguousarray(wg.T.reshape(DC, P, E).transpose(1, 0, 2)),
        "up": padded(np.concatenate([w1[:, :, :P], v1[:, :, :P], w1[:, :, P:], v1[:, :, P:]], axis=2)
                     .reshape(E, DC, P, 2 * F).transpose(0, 2, 1, 3)),
        "down_a": padded(w2[:, :P]),
        "down_b": padded(w2[:, P:]),
    }


def kernel(x, L0_tok_weight, L0_tok_lora_A, L0_tok_lora_B, L0_attn_W_Q, L0_attn_W_K, L0_attn_W_V, L0_attn_W_O, L0_attn_b_Q,
           L0_attn_b_K, L0_attn_b_V, L0_attn_b_O, L0_ffn_wg, L0_ffn_w1, L0_ffn_v1, L0_ffn_w2):
    import concourse.bacc as bacc
    import numpy as np
    from concourse.bass_utils import run_bass_kernel_spmd

    arrays = host_layout(*(np.asarray(a) for a in (
        x, L0_tok_weight, L0_tok_lora_A, L0_tok_lora_B, L0_attn_W_Q, L0_attn_W_K, L0_attn_W_V, L0_attn_W_O, L0_attn_b_Q,
        L0_attn_b_K, L0_attn_b_V, L0_attn_b_O, L0_ffn_wg, L0_ffn_w1, L0_ffn_v1, L0_ffn_w2)))
    arrays = {f"in_{name}": a for name, a in arrays.items()}
    nc = bacc.Bacc("TRN2", target_bir_lowering=False, num_devices=1)
    d = {name[3:]: nc.dram_tensor(name, a.shape, mybir.dt.from_np(a.dtype), kind="ExternalInput").ap()
         for name, a in arrays.items()}
    d["out"] = nc.dram_tensor("out_h", [T, D], F32, kind="ExternalOutput").ap()
    d["h"] = nc.dram_tensor("scratch_h", [T, D], F32).ap()
    d["z"] = nc.dram_tensor("scratch_z", [P, 2 * H, T], F16).ap()
    build(nc, d)
    r = run_bass_kernel_spmd(nc, [arrays], core_ids=[0])
    return r.results[0]["out_h"].reshape(1, T, D)
```

```python
from contextlib import ExitStack

import concourse.bass as bass
from concourse import mybir

P = 128
F32 = mybir.dt.float32
F16 = mybir.dt.float16
BF16 = mybir.dt.bfloat16
U32 = mybir.dt.uint32
I32 = mybir.dt.int32
ALU = mybir.AluOpType
ACT = mybir.ActivationFunctionType
AX = mybir.AxisListType

T = 2048
NT = T // P
D = 512
DC = D // P
H = 16
R = 64
LORA_SCALE = 128.0 / 8.0
EPS = 1e-5
E = 32
TOPK = 8
F = 192
NB = T // 512

WS = 64.0
PS = 256.0
ZS = 64.0
QS = 8.0
SCORE = 1.0 / (QS * QS * float(P) ** 0.5)


def wait(eng, sem, n):
    if isinstance(n, int) and n <= 0:
        return
    eng.wait_ge(sem, n)


def chunks(i):
    w = P * (i + 1)
    return [(0, w)] if w <= 1024 else [(0, 1024), (1024, w - 1024)]


def banks(i):
    return [(b, min(4, i + 1 - b)) for b in range(0, i + 1, 4)]


GROUPS = [0, 1, 3, 2]
TILES = [4 * g + j for g in GROUPS for j in range(4)]


def chunk_no(p):
    return sum(len(chunks(i)) for i in TILES[:p])


def bank_no(p):
    return sum(len(banks(i)) for i in TILES[:p])


NCH = chunk_no(NT)
NBK = bank_no(NT)
LONG = [i for i in TILES if len(chunks(i)) == 2]
NLONG = 2 * len(LONG)
NPB = 3 * NB


def embed_phase(nc, d, x_hi, x_lo, early):
    ident, mask, cos, sin, bqk, bv, w_in, w_hi, w_lo = early
    with ExitStack() as ctx:
        sb = lambda name, shape, dt=F32: ctx.enter_context(nc.sbuf_tensor(name, shape, dt))
        ps = lambda name, shape: ctx.enter_context(nc.psum_tensor(name, shape, F32))
        sem = lambda name: ctx.enter_context(nc.semaphore(name))
        RING = 4
        STORES = 3
        idx = sb("idx", [P, NT], I32)
        lora_b = sb("lora_b", [R, D])
        power = sb("power_a", [P, 1])
        base = [sb(f"base{i}", [P, D]) for i in range(RING)]
        rows = [sb(f"rows{i}", [P, R]) for i in range(RING)]
        rows_t = [sb(f"rows_t{i}", [R, P]) for i in range(2)]
        hid = [sb(f"hid{i}", [P, D]) for i in range(STORES)]
        norm = [sb(f"norm{i}", [P, D]) for i in range(2)]
        stats = [sb(f"stats{i}", [P, 6]) for i in range(2)]
        mv = [sb(f"mv{i}", [P, 2]) for i in range(2)]
        rstd = [sb(f"rstd{i}", [P, 1]) for i in range(2)]
        p_rows = [ps(f"p_rows{i}", [P, 512]) for i in range(2)]
        p_lora = [ps(f"p_lora{i}", [P, 512]) for i in range(2)]
        p_norm = [ps(f"p_norm{i}", [P, 512]) for i in range(2)]
        consts_in = sem("a_consts_in")
        idx_in = sem("a_idx_in")
        tables_in = sem("tables_in")
        w_loaded = sem("a_w_loaded")
        w_hi_done = sem("a_w_hi_done")
        w_lo_done = sem("a_w_lo_done")
        power_set = sem("a_power_set")
        base_in = [sem(f"a_base_in{i}") for i in range(RING)]
        rows_in = [sem(f"a_rows_in{i}") for i in range(RING)]
        rows_turned = sem("a_rows_turned")
        rows_copied = sem("a_rows_copied")
        lora_done = sem("a_lora_done")
        hid_done = sem("a_hid_done")
        hid_out = [sem(f"a_hid_out{i}") for i in range(STORES)]
        stats_done = sem("a_stats_done")
        mv_done = sem("a_mv_done")
        var_eps = sem("a_var_eps")
        rstd_done = sem("a_rstd_done")
        norm_done = sem("a_norm_done")
        norm_turned = sem("a_norm_turned")
        hi_done = sem("a_hi_done")
        lo_done = sem("a_lo_done")
        block = ctx.enter_context(nc.Block())

        @block.sync
        def _(sp):
            sp.dma_start(idx[:, :], d["idx"]).then_inc(idx_in, 16)
            sp.dma_start(ident[:, :], d["ident"]).then_inc(consts_in, 16)
            sp.dma_start(lora_b[:, :], d["lora_b"]).then_inc(consts_in, 16)
            for t in range(NT):
                sp.wait_ge(hid_done, t + 1)
                sp.dma_start(d["h"][t * P:(t + 1) * P, :], hid[t % STORES][:, :]).then_inc(hid_out[t % STORES], 16)
            for i in range(STORES):
                sp.wait_ge(hid_out[i], 16 * len(range(i, NT, STORES)))

        @block.gpsimd
        def _(pool):
            pool.memset(power[:, :], -0.5).then_inc(power_set, 1)
            pool.wait_ge(idx_in, 16)
            pool.wait_ge(power_set, 1)

            def gather(t):
                s = t % RING
                wait(pool, hid_done, t - RING + 1)
                off = bass.IndirectOffsetOnAxis(ap=idx[:, t:t + 1].bitcast(U32), axis=0)
                pool.indirect_dma_start(base[s][:, :], None, d["emb"], off).then_inc(base_in[s], 16)
                off = bass.IndirectOffsetOnAxis(ap=idx[:, t:t + 1].bitcast(U32), axis=0)
                pool.indirect_dma_start(rows[s][:, :], None, d["lora_at"], off).then_inc(rows_in[s], 16)

            for t in range(RING):
                gather(t)
            for t in range(NT):
                pool.wait_ge(var_eps, t + 1)
                wait(pool, norm_done, t - 1)
                pool.tensor_tensor(rstd[t % 2][:, :], mv[t % 2][:, 1:2], power[:, :], ALU.pow).then_inc(rstd_done, 1)
                if t + RING < NT:
                    gather(t + RING)

        @block.tensor
        def _(pe):
            pe.wait_ge(consts_in, 32)

            def turn_rows(t):
                pe.wait_ge(rows_in[t % RING], 16 * (t // RING + 1))
                wait(pe, rows_copied, t - 1)
                pe.transpose(p_rows[t % 2][0:R, 0:P], rows[t % RING][:, :], ident[:, :]).then_inc(rows_turned, 1)

            def turn_norm(t):
                pe.wait_ge(norm_done, t + 1)
                wait(pe, lo_done, t - 1)
                for c in range(DC):
                    last = pe.transpose(p_norm[t % 2][:, c * P:(c + 1) * P], norm[t % 2][:, c * P:(c + 1) * P],
                                        ident[:, :])
                last.then_inc(norm_turned, 1)

            def lora(t):
                pe.wait_ge(rows_copied, t + 1)
                wait(pe, hid_done, t - 1)
                pe.matmul(p_lora[t % 2][:, :], rows_t[t % 2][:, :], lora_b[:, :], start=True,
                          stop=True).then_inc(lora_done, 1)

            turn_rows(0)
            turn_rows(1)
            lora(0)
            for t in range(NT + 1):
                if t + 2 < NT:
                    turn_rows(t + 2)
                if t + 1 < NT:
                    lora(t + 1)
                if t:
                    turn_norm(t - 1)

        @block.vector
        def _(v):
            def copy_rows(t):
                s = t % 2
                v.wait_ge(rows_turned, t + 1)
                wait(v, lora_done, t - 1)
                v.tensor_copy(rows_t[s][:, :], p_rows[s][0:R, 0:P]).then_inc(rows_copied, 1)

            def statistics(t):
                s = t % 2
                v.wait_ge(lora_done, t + 1)
                v.wait_ge(base_in[t % RING], 16 * (t // RING + 1))
                wait(v, hid_out[t % STORES], 16 * (t // STORES))
                v.scalar_tensor_tensor(hid[t % STORES][:, :], p_lora[s][:, :], LORA_SCALE, base[t % RING][:, :], ALU.mult,
                                       ALU.add).then_inc(hid_done, 1)
                v.wait_ge(hid_done, t + 1)
                v.bn_stats(stats[s][:, :], hid[t % STORES][:, :]).then_inc(stats_done, 1)
                v.wait_ge(stats_done, t + 1)
                v.bn_aggr(mv[s][:, :], stats[s][:, :]).then_inc(mv_done, 1)
                v.wait_ge(mv_done, t + 1)
                v.tensor_scalar(mv[s][:, 1:2], mv[s][:, 1:2], EPS, None, ALU.add).then_inc(var_eps, 1)

            def normalize(t):
                s = t % 2
                v.wait_ge(rstd_done, t + 1)
                wait(v, norm_turned, t - 1)
                v.tensor_scalar(norm[s][:, :], hid[t % STORES][:, :], mv[s][:, 0:1], rstd[s][:, 0:1], ALU.subtract,
                                ALU.mult).then_inc(norm_done, 1)

            def low_half(t):
                s = t % 2
                v.wait_ge(hi_done, t + 1)
                cols = slice(t * P, (t + 1) * P)
                v.tensor_tensor(x_lo[:, :, cols], p_norm[s][:, :].rearrange("p (c n) -> p c n", c=DC),
                                x_hi[:, :, cols], ALU.subtract).then_inc(lo_done, 1)

            copy_rows(0)
            copy_rows(1)
            for t in range(NT + 2):
                if 1 <= t <= NT:
                    normalize(t - 1)
                if t < NT:
                    statistics(t)
                if t + 2 < NT:
                    copy_rows(t + 2)
                if t >= 2:
                    low_half(t - 2)
                if t == NT // 2 + 2:
                    v.wait_ge(w_hi_done, 1)
                    v.scalar_tensor_tensor(w_lo[:, :, :, :].rearrange("p m c e -> p (m c e)"),
                                           w_in[:, :, :, :].rearrange("p m c e -> p (m c e)"), WS,
                                           w_hi[:, :, :, :].rearrange("p m c e -> p (m c e)"), ALU.mult,
                                           ALU.subtract).then_inc(w_lo_done, 1)

        @block.scalar
        def _(act):
            act.wait_ge(norm_done, 1)
            act.dma_start(w_in[:, :, :, :], d["wqkv"][0]).then_inc(w_loaded, 16)
            for dst, src in ((mask[:, :], d["mask"]), (cos[:, :], d["cos"]), (sin[:, :], d["sin"]), (bqk[:, :, :], d["bqk"]),
                             (bv[0][:, :], d["bv"][0:1, :].to_broadcast([P, P]))):
                act.dma_start(dst, src).then_inc(tables_in, 16)
            for t in range(NT):
                if t == NT // 2:
                    act.wait_ge(w_loaded, 16)
                    act.activation(w_hi[:, :, :, :], w_in[:, :, :, :], ACT.Copy, scale=WS).then_inc(w_hi_done, 1)
                act.wait_ge(norm_turned, t + 1)
                act.activation(x_hi[:, :, t * P:(t + 1) * P], p_norm[t % 2][:, :].rearrange("p (c n) -> p c n", c=DC),
                               ACT.Copy).then_inc(hi_done, 1)
            act.wait_ge(tables_in, 80)


def attention_phase(nc, d, x_hi, x_lo, early):
    ident, mask, cos, sin, bqk, bv, w_in, w_hi, w_lo = early
    with ExitStack() as ctx:
        sb = lambda name, shape, dt=F32: ctx.enter_context(nc.sbuf_tensor(name, shape, dt))
        ps = lambda name, shape: ctx.enter_context(nc.psum_tensor(name, shape, F32))
        sem = lambda name: ctx.enter_context(nc.semaphore(name))
        mask16 = sb("mask16", [P, P], BF16)
        ones = sb("ones", [P, P])
        by_cos = [sb(f"by_cos{i}", [P, 512]) for i in range(2)]
        by_sin = [sb(f"by_sin{i}", [P, 512]) for i in range(2)]
        turned = [sb(f"turned{i}", [P, 512]) for i in range(2)]
        q_hi = [sb(f"q_hi{i}", [P, T], F16) for i in range(2)]
        q_lo = [sb(f"q_lo{i}", [P, T], F16) for i in range(2)]
        k_hi = [sb(f"k_hi{i}", [P, T], F16) for i in range(2)]
        k_lo = [sb(f"k_lo{i}", [P, T], F16) for i in range(2)]
        v_hi = [sb(f"v_hi{i}", [P, NT, P], F16) for i in range(2)]
        v_lo = [sb(f"v_lo{i}", [P, NT, P], F16) for i in range(2)]
        a = [sb(f"a{i}", [P, P * (13 + i)]) for i in range(4)]
        sign = [sb(f"sign{i}", [P, P * (13 + i)], BF16) for i in range(4)]
        bias = sb("bias", [P, 4])
        parts = sb("parts", [P, 4, 2])
        total = sb("total", [P, 4])
        total_eps = sb("total_eps", [P, 4])
        inv_total = sb("inv_total", [P, 4])
        diag = sb("diag", [P, 4, P])
        inv_row = sb("inv_row", [P, 512])
        wt_hi = sb("wt_hi", [P, NT, 512], F16)
        wt_lo = sb("wt_lo", [P, NT, 512], F16)
        z = sb("z", [P, 512])
        z_half = sb("z_half", [P, 2, 512], F16)
        p_score = [ps(f"p_score{i}", [P, 1024]) for i in range(2)]
        p_turn = [ps(f"p_turn{i}", [P, 512]) for i in range(2)]
        p_proj = ps("p_proj", [P, 512])
        p_z = ps("p_z", [P, 512])

        consts_set = sem("b_consts_set")
        mask_done = sem("mask_done")
        w_loaded = sem("w_loaded")
        bias_scaled = sem("bias_scaled")
        w_hi_done = sem("w_hi_done")
        w_lo_done = sem("w_lo_done")
        proj_done = sem("proj_done")
        cos_done = sem("cos_done")
        proj_read = sem("proj_read")
        turned_done = sem("turned_done")
        proj_hi_done = sem("proj_hi_done")
        proj_split = sem("proj_split")
        scores_done = sem("scores_done")
        masked = sem("masked")
        sign_masked = sem("sign_masked")
        part_done = sem("part_done")
        bias_done = sem("bias_done")
        abs_done = sem("abs_done")
        sign_done = sem("sign_done")
        exp_done = sem("exp_done")
        signed_done = sem("signed_done")
        total_done = sem("total_done")
        eps_added = sem("eps_added")
        inv_done = sem("inv_done")
        diag_done = sem("diag_done")
        inv_row_done = sem("inv_row_done")
        inv_row_copied = sem("inv_row_copied")
        wt_turned = sem("wt_turned")
        wt_hi_done = sem("wt_hi_done")
        wt_split = sem("wt_split")
        pv_done = sem("pv_done")
        z_read = sem("z_read")
        z_hi_done = sem("z_hi_done")
        z_split = sem("z_split")
        z_out = sem("z_out")
        block = ctx.enter_context(nc.Block())

        LAG = 3
        FILL = 6
        SPLIT_AT = FILL + NPB - NT
        WARM = H // 2 - 1

        def heads(eng, step):
            for i in range(NT):
                step(0, 0, i, None)
            with eng.Fori(0, WARM) as pair:
                for u in range(2):
                    for i in range(NT):
                        step(pair * 2 + (1 + u), (1 + u) % 2, i, True)
            for i in range(NT + LAG + 2):
                step(H - 1, (H - 1) % 2, i, False)

        def lagged(h, i, by, prev):
            if i - by >= NT:
                return None
            if i - by >= 0:
                return h, 0, i - by
            return None if prev is None else (h - 1, 1, i - by + NT)

        def group_at(h, i, phase, prev):
            g, rest = divmod(i - 3 - phase, 4)
            if rest or g > 3:
                return None
            if g >= 0:
                return h, 0, g
            return None if prev is None else (h - 1, 1, g + 4)

        def filler_at(h, i, by, prev):
            k = i - FILL - by
            if prev is not False and 0 <= k < NPB:
                return h + 1, 1, k
            if prev is not None and i < NT and 0 <= k + NT < NPB:
                return h, 0, k + NT
            return None

        @block.sync
        def _(sp):
            def load(n, parity):
                wait(sp, w_lo_done, n - 1)
                sp.dma_start(w_in[:, :, :, :], d["wqkv"][n] if isinstance(n, int) else
                             d["wqkv"][bass.ds(n, 1)].rearrange("a p m c e -> (a p) m c e")).then_inc(w_loaded, 16)
                sp.dma_start(bv[parity][:, :], (d["bv"][n:n + 1, :] if isinstance(n, int) else
                             d["bv"][bass.ds(n, 1), :]).to_broadcast([P, P])).then_inc(w_loaded, 16)

            load(1, 1)

            def step(h, parity, i, prev):
                if i == 2 and prev is not False:
                    load(h + 2, parity)
                got = group_at(h, i, LAG + 2, prev)
                if got:
                    gh, _, g = got
                    sp.wait_ge(z_split, 4 * gh + g + 1)
                    rows = slice(2 * gh, 2 * gh + 2) if isinstance(gh, int) else bass.ds(gh * 2, 2)
                    cols = slice(GROUPS[g] * 512, (GROUPS[g] + 1) * 512)
                    sp.dma_start(d["z"][:, rows, cols], z_half[:, :, :]).then_inc(z_out, 16)

            heads(sp, step)
            sp.wait_ge(z_out, 16 * 4 * H)
            sp.wait_ge(w_loaded, 32 * H)

        @block.tensor
        def _(pe):
            pe.wait_ge(consts_set, 1)

            def project(h, parity, k, quarters):
                b, what = k // 3, k % 3
                if 0 in quarters:
                    if k == 0:
                        wait(pe, w_lo_done, h)
                    wait(pe, proj_read, NPB * h + k)
                for r in quarters:
                    if what < 2:
                        for n, (wx, xx) in enumerate(((w_hi, x_hi), (w_lo, x_hi), (w_hi, x_lo))):
                            last = pe.matmul(p_proj[:, :], wx[:, what, r, :], xx[:, r, b * 512:(b + 1) * 512],
                                             start=(r == 0 and n == 0), stop=(r == DC - 1 and n == 2))
                        continue
                    cols = slice(b * 512 + r * P, b * 512 + (r + 1) * P)
                    for c in range(DC):
                        for n, (wx, xx) in enumerate(((w_hi, x_hi), (w_lo, x_hi), (w_hi, x_lo))):
                            last = pe.matmul(p_proj[:, r * P:(r + 1) * P], xx[:, c, cols], wx[:, what, c, :],
                                             start=(c == 0 and n == 0), stop=(c == DC - 1 and n == 2))
                if 3 in quarters:
                    last.then_inc(proj_done, 1)

            def scores(h, parity, p, quarter):
                i = TILES[p]
                if i % 4 == 0 and quarter == 0:
                    pe.wait_ge(proj_split, NPB * h + 3 * (i // 4) + 2)
                c0 = 512 * quarter
                m = min(512, P * (i + 1) - c0)
                if m <= 0:
                    return
                n = quarter // 2
                no = NCH * h + chunk_no(p) + n
                s = (chunk_no(p) + n) % 2
                if quarter % 2 == 0:
                    wait(pe, sign_done, no - 1)
                o = c0 % 1024
                for x, (qx, kx) in enumerate(((q_hi, k_hi), (q_hi, k_lo), (q_lo, k_hi))):
                    last = pe.matmul(p_score[s][:, o:o + m], qx[parity][:, i * P:(i + 1) * P],
                                     kx[parity][:, c0:c0 + m], start=(x == 0), stop=(x == 2))
                if o + m == chunks(i)[n][1]:
                    last.then_inc(scores_done, 1)

            def turn(h, p, n):
                i = TILES[p]
                if n >= len(banks(i)):
                    return
                b, m = banks(i)[n]
                no = NBK * h + bank_no(p) + n
                s = (bank_no(p) + n) % 2
                pe.wait_ge(signed_done, no + 1)
                wait(pe, wt_split, no - 1)
                for j in range(m):
                    last = pe.transpose(p_turn[s][:, j * P:(j + 1) * P], a[i % 4][:, (b + j) * P:(b + j + 1) * P],
                                        ident[:, :])
                last.then_inc(wt_turned, 1)

            def row_of_inverses(h, g):
                pe.wait_ge(diag_done, 4 * h + g + 1)
                wait(pe, z_read, 4 * h + g)
                pe.matmul(p_z[:, :], ones[:, :], diag[:, :, :].rearrange("p j n -> p (j n)"), start=True,
                          stop=True).then_inc(inv_row_done, 1)

            def values(h, parity, q, quarter):
                g = GROUPS[q]
                if quarter > g:
                    return
                if quarter == 0:
                    pe.wait_ge(inv_row_copied, 4 * h + q + 1)
                    pe.wait_ge(proj_split, NPB * h + 3 * g + 3)
                    pe.wait_ge(wt_split, NBK * h + bank_no(4 * q + 4))
                for b in range(4 * quarter, 4 * quarter + 4):
                    o = max(0, b - 4 * g) * P
                    for p, (vx, wx) in enumerate(((v_hi, wt_hi), (v_hi, wt_lo), (v_lo, wt_hi))):
                        last = pe.matmul(p_z[:, o:], vx[parity][:, b, :], wx[:, b, o:], start=(b == 0 and p == 0),
                                         stop=(b == 4 * g + 3 and p == 2))
                if quarter == g:
                    last.then_inc(pv_done, 1)

            for k in range(NPB):
                project(0, 0, k, range(4))

            def step(h, parity, i, prev):
                filler = filler_at(h, i, 0, prev)
                fill = lambda quarters: project(filler[0], (parity + filler[1]) % 2, filler[2], quarters) if filler else None
                for n in range(4):
                    if i < NT:
                        scores(h, parity, i, n)
                    if got := group_at(h, i, LAG + 1, prev):
                        values(got[0], (parity + got[1]) % 2, got[2], n)
                    if n == 2:
                        if got := group_at(h, i, LAG, prev):
                            row_of_inverses(got[0], got[2])
                        fill((0,))
                    if got := lagged(h, i, LAG, prev):
                        turn(got[0], got[2], n)
                    if n == 2:
                        fill((1,))
                fill((2, 3))

            heads(pe, step)

        @block.vector
        def _(v):
            v.memset(ones[:, :], 1.0).then_inc(consts_set, 1)
            v.tensor_scalar(bqk[:, :, :], bqk[:, :, :], WS, None, ALU.mult).then_inc(bias_scaled, 1)
            v.wait_ge(bias_scaled, 1)
            v.wait_ge(consts_set, 1)

            def w_low(n):
                v.wait_ge(w_hi_done, n)
                v.scalar_tensor_tensor(w_lo[:, :, :, :].rearrange("p m c e -> p (m c e)"),
                                       w_in[:, :, :, :].rearrange("p m c e -> p (m c e)"), WS,
                                       w_hi[:, :, :, :].rearrange("p m c e -> p (m c e)"), ALU.mult,
                                       ALU.subtract).then_inc(w_lo_done, 1)

            def read_projection(h, parity, k):
                no = NPB * h + k
                b, what = k // 3, k % 3
                v.wait_ge(proj_done, no + 1)
                wait(v, proj_split, no - 1)
                if what == 2:
                    v.scalar_tensor_tensor(
                        by_cos[k % 2][:, :].rearrange("p (t e) -> p t e", t=4), p_proj[:, :].rearrange("p (t e) -> p t e", t=4),
                        1.0 / WS, bv[parity][:, :].rearrange("p (a e) -> p a e", a=1).to_broadcast([P, 4, P]), ALU.mult,
                        ALU.add).then_inc(proj_read, 1)
                    return
                cols = slice(b * 512, (b + 1) * 512)
                v.scalar_tensor_tensor(by_cos[k % 2][:, :], p_proj[:, :], bqk_at(0, P, what, h), cos[:, cols], ALU.add,
                                       ALU.mult).then_inc(cos_done, 1)
                v.scalar_tensor_tensor(by_sin[k % 2][0:64, :], p_proj[64:P, :], bqk_at(64, P, what, h), sin[0:64, cols],
                                       ALU.add, ALU.mult).then_inc(cos_done, 1)
                v.scalar_tensor_tensor(by_sin[k % 2][64:P, :], p_proj[0:64, :], bqk_at(0, 64, what, h), sin[64:P, cols],
                                       ALU.add, ALU.mult).then_inc(proj_read, 1)

            def bqk_at(p0, p1, what, h):
                if isinstance(h, int):
                    return bqk[p0:p1, what, h:h + 1]
                return bqk[p0:p1, what, bass.ds(h, 1)]

            def maximum_first(h, p):
                i = TILES[p]
                if len(chunks(i)) == 1:
                    return
                v.wait_ge(abs_done, NCH * h + chunk_no(p) + 1)
                v.tensor_reduce(parts[:, i % 4, 0:1], a[i % 4][:, 0:1024], AX.X, ALU.max).then_inc(part_done, 1)

            def maximum(h, p):
                i = TILES[p]
                v.wait_ge(abs_done, NCH * h + chunk_no(p + 1))
                tri = a[i % 4][:, P * i:P * (i + 1)]
                v.tensor_tensor(tri, tri, mask[:, :], ALU.mult).then_inc(masked, 1)
                v.wait_ge(masked, NT * h + p + 1)
                if len(chunks(i)) == 2:
                    v.tensor_reduce(parts[:, i % 4, 1:2], a[i % 4][:, 1024:P * (i + 1)], AX.X, ALU.max).then_inc(part_done, 1)
                    v.wait_ge(part_done, NLONG * h + 2 * LONG.index(i) + 2)
                    v.tensor_reduce(bias[:, i % 4:i % 4 + 1], parts[:, i % 4, :], AX.X, ALU.max,
                                    negate=True).then_inc(bias_done, 1)
                    return
                v.tensor_reduce(bias[:, i % 4:i % 4 + 1], a[i % 4][:, 0:P * (i + 1)], AX.X, ALU.max,
                                negate=True).then_inc(bias_done, 1)

            def sum_up(h, p):
                i = TILES[p]
                v.wait_ge(signed_done, NBK * h + bank_no(p + 1))
                v.tensor_reduce(total[:, i % 4:i % 4 + 1], a[i % 4][:, 0:P * (i + 1)], AX.X, ALU.add,
                                apply_absolute_value=True).then_inc(total_done, 1)

            def inverses(h, g):
                m = 4 * h + g
                v.wait_ge(total_done, NT * h + 4 * g + 4)
                v.tensor_scalar(total_eps[:, :], total[:, :], 1e-6, None, ALU.add).then_inc(eps_added, 1)
                v.wait_ge(eps_added, m + 1)
                v.reciprocal(inv_total[:, :], total_eps[:, :]).then_inc(inv_done, 1)
                v.wait_ge(inv_done, m + 1)
                wait(v, inv_row_done, m)
                v.scalar_tensor_tensor(diag[:, :, :],
                                       ident[:, :].rearrange("p (a n) -> p a n", a=1).to_broadcast([P, 4, P]), ZS / PS,
                                       inv_total[:, :].rearrange("p (j a) -> p j a", a=1).to_broadcast([P, 4, P]),
                                       ALU.mult, ALU.mult).then_inc(diag_done, 1)

            def low_halves(h, p, which):
                i = TILES[p]
                for n in which:
                    if n >= len(banks(i)):
                        return
                    b, m = banks(i)[n]
                    no = NBK * h + bank_no(p) + n
                    v.wait_ge(wt_hi_done, no + 1)
                    cols = slice(i % 4 * P, (i % 4 + 1) * P)
                    v.scalar_tensor_tensor(
                        wt_lo[:, b:b + m, cols], p_turn[(bank_no(p) + n) % 2][:, 0:m * P].rearrange("p (j n) -> p j n", j=m),
                        PS, wt_hi[:, b:b + m, cols], ALU.mult, ALU.subtract).then_inc(wt_split, 1)

            def read_z(h, g):
                m = 4 * h + g
                v.wait_ge(pv_done, m + 1)
                wait(v, z_split, m)
                v.tensor_tensor(z[:, :], p_z[:, :], inv_row[:, :], ALU.mult).then_inc(z_read, 1)

            for k in range(NPB):
                read_projection(0, 0, k)
            w_low(1)

            def step(h, parity, i, prev):
                if got := filler_at(h, i, 1, prev):
                    read_projection(got[0], (parity + got[1]) % 2, got[2])
                behind = lagged(h, i, LAG, prev)
                if behind:
                    low_halves(behind[0], behind[2], (0, 1))
                if got := lagged(h, i, 2, prev):
                    sum_up(got[0], got[2])
                if got := group_at(h, i, 2, prev):
                    inverses(got[0], got[2])
                if behind:
                    low_halves(behind[0], behind[2], (2, 3))
                if got := group_at(h, i, LAG + 2, prev):
                    read_z(got[0], got[2])
                if i < NT:
                    maximum_first(h, i)
                    maximum(h, i)
                if i == SPLIT_AT and prev is True:
                    w_low(h + 1)

            heads(v, step)

        @block.scalar
        def _(act):
            def w_high(n):
                act.wait_ge(w_loaded, 32 * n)
                wait(act, proj_done, NPB * n)
                act.activation(w_hi[:, :, :, :], w_in[:, :, :, :], ACT.Copy, scale=WS).then_inc(w_hi_done, 1)

            def proj_high(h, parity, k):
                no = NPB * h + k
                b, what = k // 3, k % 3
                if what == 2:
                    act.wait_ge(proj_read, no + 1)
                    act.activation(v_hi[parity][:, 4 * b:4 * b + 4, :], by_cos[k % 2][:, :].rearrange("p (t e) -> p t e", t=4),
                                   ACT.Copy).then_inc(proj_hi_done, 1)
                else:
                    act.wait_ge(turned_done, 2 * NB * h + 2 * b + what + 1)
                    act.activation((q_hi, k_hi)[what][parity][:, b * 512:(b + 1) * 512], turned[k % 2][:, :],
                                   ACT.Copy).then_inc(proj_hi_done, 1)

            def abs_and_sign(h, p, n):
                i = TILES[p]
                if n >= len(chunks(i)):
                    return
                c0, w = chunks(i)[n]
                no = NCH * h + chunk_no(p) + n
                s = (chunk_no(p) + n) % 2
                if n == 0:
                    wait(act, total_done, NT * h + p - 3)
                act.wait_ge(scores_done, no + 1)
                act.activation(a[i % 4][:, c0:c0 + w], p_score[s][:, 0:w], ACT.Abs, scale=SCORE).then_inc(abs_done, 1)
                act.activation(sign[i % 4][:, c0:c0 + w], p_score[s][:, 0:w], ACT.Sign).then_inc(sign_done, 1)

            def exponentials(h, p):
                i = TILES[p]
                act.wait_ge(bias_done, NT * h + p + 1)
                act.activation(a[i % 4][:, 0:P * (i + 1)], a[i % 4][:, 0:P * (i + 1)], ACT.Exp,
                               bias=bias[:, i % 4:i % 4 + 1]).then_inc(exp_done, 1)

            def high_halves(h, p, which):
                i = TILES[p]
                for n in which:
                    if n >= len(banks(i)):
                        return
                    b, m = banks(i)[n]
                    no = NBK * h + bank_no(p) + n
                    act.wait_ge(wt_turned, no + 1)
                    act.activation(wt_hi[:, b:b + m, i % 4 * P:(i % 4 + 1) * P],
                                   p_turn[(bank_no(p) + n) % 2][:, 0:m * P].rearrange("p (j n) -> p j n", j=m), ACT.Copy,
                                   scale=PS).then_inc(wt_hi_done, 1)

            def copy_inverses(h, g):
                m = 4 * h + g
                act.wait_ge(inv_row_done, m + 1)
                wait(act, z_read, m)
                act.activation(inv_row[:, :], p_z[:, :], ACT.Copy).then_inc(inv_row_copied, 1)

            def z_high(h, g):
                m = 4 * h + g
                act.wait_ge(z_read, m + 1)
                wait(act, z_out, 16 * m)
                act.activation(z_half[:, 0, :], z[:, :], ACT.Copy).then_inc(z_hi_done, 1)

            for k in range(NPB):
                proj_high(0, 0, k)
            w_high(1)

            def step(h, parity, i, prev):
                if got := group_at(h, i, LAG + 1, prev):
                    copy_inverses(got[0], got[2])
                behind = lagged(h, i, LAG, prev)
                if behind:
                    high_halves(behind[0], behind[2], (0, 1))
                if i < NT:
                    abs_and_sign(h, i, 0)
                if got := lagged(h, i, 1, prev):
                    exponentials(got[0], got[2])
                if got := filler_at(h, i, 1, prev):
                    proj_high(got[0], (parity + got[1]) % 2, got[2])
                if behind:
                    high_halves(behind[0], behind[2], (2, 3))
                if i < NT:
                    abs_and_sign(h, i, 1)
                if got := group_at(h, i, LAG + 2, prev):
                    z_high(got[0], got[2])
                if i == SPLIT_AT and prev is True:
                    w_high(h + 1)

            heads(act, step)

        @block.gpsimd
        def _(pool):
            pool.tensor_copy(mask16[:, :], mask[:, :]).then_inc(mask_done, 1)
            pool.wait_ge(mask_done, 1)

            def rotate(h, k):
                no = NPB * h + k
                b, what = k // 3, k % 3
                if what == 2:
                    return
                pool.wait_ge(proj_read, no + 1)
                pool.wait_ge(cos_done, 2 * (2 * NB * h + 2 * b + what + 1))
                pool.tensor_tensor(turned[k % 2][:, :], by_cos[k % 2][:, :], by_sin[k % 2][:, :], ALU.add).then_inc(turned_done, 1)

            def proj_low(h, parity, k):
                no = NPB * h + k
                b, what = k // 3, k % 3
                pool.wait_ge(proj_hi_done, no + 1)
                if what == 2:
                    pool.tensor_tensor(v_lo[parity][:, 4 * b:4 * b + 4, :].rearrange("p t e -> p (t e)"), by_cos[k % 2][:, :],
                                       v_hi[parity][:, 4 * b:4 * b + 4, :].rearrange("p t e -> p (t e)"),
                                       ALU.subtract).then_inc(proj_split, 1)
                else:
                    pool.wait_ge(turned_done, 2 * NB * h + 2 * b + what + 1)
                    cols = slice(b * 512, (b + 1) * 512)
                    pool.tensor_tensor((q_lo, k_lo)[what][parity][:, cols], turned[k % 2][:, :],
                                       (q_hi, k_hi)[what][parity][:, cols], ALU.subtract).then_inc(proj_split, 1)

            def put_sign(h, p):
                i = TILES[p]
                pool.wait_ge(sign_done, NCH * h + chunk_no(p + 1))
                tri = sign[i % 4][:, P * i:P * (i + 1)]
                pool.tensor_tensor(tri, tri, mask16[:, :], ALU.mult).then_inc(sign_masked, 1)
                pool.wait_ge(exp_done, NT * h + p + 1)
                pool.wait_ge(sign_masked, NT * h + p + 1)
                for b, m in banks(i):
                    cols = slice(b * P, (b + m) * P)
                    pool.tensor_tensor(a[i % 4][:, cols], a[i % 4][:, cols], sign[i % 4][:, cols],
                                       ALU.mult).then_inc(signed_done, 1)

            def z_low(h, g):
                pool.wait_ge(z_hi_done, 4 * h + g + 1)
                pool.tensor_tensor(z_half[:, 1, :], z[:, :], z_half[:, 0, :], ALU.subtract).then_inc(z_split, 1)

            for k in range(NPB):
                rotate(0, k)
                proj_low(0, 0, k)

            def step(h, parity, i, prev):
                filler = filler_at(h, i, 1, prev)
                if filler:
                    rotate(filler[0], filler[2])
                if got := lagged(h, i, 1, prev):
                    put_sign(got[0], got[2])
                if filler:
                    proj_low(filler[0], (parity + filler[1]) % 2, filler[2])
                if got := group_at(h, i, LAG + 2, prev):
                    z_low(got[0], got[2])

            heads(pool, step)


def output_phase(nc, d, x_hi, x_lo, acc, gate, first):
    up_in, up_hi, up_lo, down_in, down_hi, down_lo = first
    with ExitStack() as ctx:
        sb = lambda name, shape, dt=F32: ctx.enter_context(nc.sbuf_tensor(name, shape, dt))
        ps = lambda name, shape: ctx.enter_context(nc.psum_tensor(name, shape, F32))
        sem = lambda name: ctx.enter_context(nc.semaphore(name))
        PART = 2
        ident = sb("ident_c", [P, P])
        power = sb("power_c", [P, 1])
        bo = sb("bo", [P, D])
        wg_in = sb("wg_in", [P, DC, E])
        wg_hi = sb("wg_hi", [P, DC, E], F16)
        wg_lo = sb("wg_lo", [P, DC, E], F16)
        wo_hi = sb("wo_hi", [P, H, D], F16)
        wo_lo = sb("wo_lo", [P, H, D], F16)
        zs = [sb(f"zs{i}", [P, 2 * H, 512], F16) for i in range(2)]
        hid = [sb(f"hid_c{i}", [P, D]) for i in range(2)]
        norm = [sb(f"norm_c{i}", [P, D]) for i in range(2)]
        xt_hi = [sb(f"xt_hi{i}", [P, DC, P], F16) for i in range(2)]
        xt_lo = [sb(f"xt_lo{i}", [P, DC, P], F16) for i in range(2)]
        stats = sb("stats_c", [P, 6])
        mv = sb("mv_c", [P, 2])
        rstd = sb("rstd_c", [P, 1])
        top_bias = sb("top_bias", [P, 1])
        e_sum = sb("e_sum", [P, 1])
        e_inv = sb("e_inv", [P, 1])
        expd = sb("expd", [P, E])
        probs = sb("probs", [P, E])
        top8 = sb("top8", [P, 8])
        rest = sb("rest", [P, E])
        chosen = sb("chosen", [P, E])
        chosen_sum = sb("chosen_sum", [P, 1])
        chosen_inv = sb("chosen_inv", [P, 1])
        p_out = [ps(f"p_out{i}", [P, 512]) for i in range(2)]
        p_norm = [ps(f"p_norm_c{i}", [P, 512]) for i in range(2)]
        p_logit = ps("p_logit", [P, 512])
        consts_in = sem("c_consts_in")
        power_set = sem("c_power_set")
        wo_loaded = [sem(f"wo_loaded{i}") for i in range(H // PART)]
        wo_hi_done = sem("wo_hi_done")
        wo_lo_done = sem("wo_lo_done")
        zs_in = [[sem(f"zs_in{i}_{q}") for q in range(H // PART)] for i in range(2)]
        hid_in = [sem(f"c_hid_in{i}") for i in range(2)]
        biased = sem("c_biased")
        out_done = sem("out_done")
        acc_done = sem("acc_done")
        kept = sem("kept")
        stats_done = sem("c_stats_done")
        mv_done = sem("c_mv_done")
        var_eps = sem("c_var_eps")
        rstd_done = sem("c_rstd_done")
        norm_done = sem("c_norm_done")
        norm_turned = sem("c_norm_turned")
        hi_done = sem("c_hi_done")
        lo_done = sem("c_lo_done")
        x_kept = sem("x_kept")
        logits_done = sem("logits_done")
        top_bias_done = sem("top_bias_done")
        exp_done = sem("c_exp_done")
        e_inv_done = sem("e_inv_done")
        probs_done = sem("probs_done")
        top8_done = sem("top8_done")
        rest_done = sem("rest_done")
        chosen_done = sem("chosen_done")
        chosen_inv_done = sem("chosen_inv_done")
        gate_done = sem("gate_done")
        w_loaded = sem("c_w_loaded")
        w_hi_done = sem("c_w_hi_done")
        w_lo_done = sem("c_w_lo_done")
        block = ctx.enter_context(nc.Block())
        PAIRS = NB // 2
        FIRST = 10

        def tiles(eng, step):
            with eng.Fori(0, PAIRS) as pair:
                for n in range(8):
                    step(pair * 8 + n, n, pair)

        @block.sync
        def _(sp):
            sp.dma_start(ident[:, :], d["ident"]).then_inc(consts_in, 16)
            sp.dma_start(wg_in[:, :, :], d["wg"]).then_inc(consts_in, 16)
            sp.dma_start(bo[:, :], d["bo"].to_broadcast([P, D])).then_inc(consts_in, 16)

            def load_z(t, n, pair):
                if n % 4 == 0:
                    sp.wait_ge(out_done, t + 4)
                    for q in range(H // PART):
                        rows = slice(2 * PART * q, 2 * PART * (q + 1))
                        sp.dma_start(zs[n // 4][:, rows, :],
                                     d["z"][:, rows, bass.ds(pair * 1024 + n // 4 * 512, 512)]).then_inc(zs_in[n // 4][q], 16)

            tiles(sp, load_z)

        @block.gpsimd
        def _(pool):
            pool.memset(power[:, :], -0.5).then_inc(power_set, 1)
            pool.sem_inc(kept, 2)
            pool.wait_ge(power_set, 1)
            pool.wait_ge(consts_in, 48)

            def step(t, n, pair):
                s = n % 2
                pool.wait_ge(norm_done, t + 1)
                pool.wait_ge(kept, t + 1)
                pool.dma_start(hid[s][:, :], d["h"][bass.ds(t * P, P), :]).then_inc(hid_in[s], 16)
                pool.wait_ge(hid_in[s], 16 * (pair * 4 + (n // 2 + 1)))
                pool.tensor_tensor(hid[s][:, :], hid[s][:, :], bo[:, :], ALU.add).then_inc(biased, 1)
                pool.wait_ge(var_eps, t + 1)
                pool.tensor_tensor(rstd[:, :], mv[:, 1:2], power[:, :], ALU.pow).then_inc(rstd_done, 1)
                pool.tensor_copy(acc[:, bass.ds(t, 1), :].rearrange("p a n -> p (a n)"), hid[s][:, :]).then_inc(kept, 1)

            tiles(pool, step)

        @block.tensor
        def _(pe):
            pe.sem_inc(out_done, 8)
            pe.wait_ge(consts_in, 48)
            def output(t, n, pair, part):
                if part == 0:
                    pe.wait_ge(acc_done, t + 1)
                cols = slice(n % 4 * P, (n % 4 + 1) * P)
                for h in (range(FIRST), range(FIRST, H))[part]:
                    if n % 4 == 0 and h % PART == 0:
                        pe.wait_ge(zs_in[n // 4][h // PART], 16 * (pair + 1))
                    if n == 0 and h % PART == 0:
                        pe.wait_ge(wo_lo_done, h // PART + 2)
                    for p, (half, w) in enumerate(((0, wo_hi), (0, wo_lo), (1, wo_hi))):
                        last = pe.matmul(p_out[n % 2][:, :], zs[n // 4][:, 2 * h + half, cols], w[:, h, :],
                                         start=(h == 0 and p == 0), stop=(h == H - 1 and p == 2))
                if part == 1:
                    last.then_inc(out_done, 1)

            def turn(t, s):
                pe.wait_ge(norm_done, t + 3)
                for c in range(DC):
                    last = pe.transpose(p_norm[s][:, c * P:(c + 1) * P], norm[s][:, c * P:(c + 1) * P], ident[:, :])
                last.then_inc(norm_turned, 1)

            def logits(t, s):
                pe.wait_ge(x_kept, t + 1)
                pe.wait_ge(gate_done, t + 1)
                for c in range(DC):
                    for p, (xx, w) in enumerate(((xt_hi, wg_hi), (xt_hi, wg_lo), (xt_lo, wg_hi), (xt_lo, wg_lo))):
                        last = pe.matmul(p_logit[:, 0:E], xx[s][:, c, :], w[:, c, :], start=(c == 0 and p == 0),
                                         stop=(c == DC - 1 and p == 3))
                last.then_inc(logits_done, 1)

            with pe.Fori(0, PAIRS) as pair:
                for n in range(9):
                    t = pair * 8 + n
                    if n < 8:
                        output(t, n, pair, 0)
                    if n:
                        turn(pair * 8 + (n - 1), (n - 1) % 2)
                    if n < 8:
                        output(t, n, pair, 1)
                    if n:
                        logits(pair * 8 + (n - 1), (n - 1) % 2)

        @block.vector
        def _(v):
            v.sem_inc(acc_done, 2)
            v.sem_inc(norm_done, 2)
            v.sem_inc(gate_done, 1)
            v.wait_ge(consts_in, 48)
            v.wait_ge(wo_hi_done, 1)
            v.scalar_tensor_tensor(wg_lo[:, :, :], wg_in[:, :, :], WS, wg_hi[:, :, :], ALU.mult,
                                   ALU.subtract).then_inc(wo_lo_done, 1)
            for n in range(H // PART):
                v.wait_ge(wo_hi_done, n + 2)
                v.scalar_tensor_tensor(wo_lo[:, n * PART:(n + 1) * PART, :], acc[:, n * PART:(n + 1) * PART, :], WS,
                                       wo_hi[:, n * PART:(n + 1) * PART, :], ALU.mult, ALU.subtract).then_inc(wo_lo_done, 1)
            v.wait_ge(w_hi_done, 1)
            v.scalar_tensor_tensor(up_lo[:, :, :], up_in[:, :, :], WS, up_hi[:, :, :], ALU.mult, ALU.subtract)
            v.scalar_tensor_tensor(down_lo[:, :, :], down_in[:, :, :], WS, down_hi[:, :, :], ALU.mult,
                                   ALU.subtract).then_inc(w_lo_done, 1)

            def step(t, n, pair):
                s = n % 2
                v.wait_ge(out_done, t + 9)
                v.wait_ge(biased, t + 1)
                row = hid[s][:, :]
                v.scalar_tensor_tensor(row, p_out[s][:, :], 1.0 / (WS * ZS), hid[s][:, :], ALU.mult,
                                       ALU.add).then_inc(acc_done, 1)
                v.wait_ge(consts_in, 48)
                v.wait_ge(acc_done, t + 3)
                v.bn_stats(stats[:, :], row).then_inc(stats_done, 1)
                v.wait_ge(consts_in, 48)
                v.wait_ge(stats_done, t + 1)
                v.bn_aggr(mv[:, :], stats[:, :]).then_inc(mv_done, 1)
                v.wait_ge(mv_done, t + 1)
                v.tensor_scalar(mv[:, 1:2], mv[:, 1:2], EPS, None, ALU.add).then_inc(var_eps, 1)
                v.wait_ge(rstd_done, t + 1)
                v.tensor_scalar(norm[s][:, :], row, mv[:, 0:1], rstd[:, 0:1], ALU.subtract, ALU.mult).then_inc(norm_done, 1)
                v.wait_ge(hi_done, t + 1)
                v.tensor_tensor(xt_lo[s][:, :, :], p_norm[s][:, :].rearrange("p (c n) -> p c n", c=DC), xt_hi[s][:, :, :],
                                ALU.subtract).then_inc(lo_done, 1)
                v.wait_ge(lo_done, t + 1)
                cols = bass.ds(t * P, P)
                v.tensor_copy(x_hi[:, :, cols], xt_hi[s][:, :, :])
                v.tensor_copy(x_lo[:, :, cols], xt_lo[s][:, :, :]).then_inc(x_kept, 1)
                v.wait_ge(logits_done, t + 1)
                v.tensor_reduce(top_bias[:, :], p_logit[:, 0:E], AX.X, ALU.max, negate=True).then_inc(top_bias_done, 1)
                v.wait_ge(top_bias_done, 2 * t + 1)
                v.tensor_scalar(top_bias[:, :], top_bias[:, :], 1.0 / WS, None, ALU.mult).then_inc(top_bias_done, 1)
                v.wait_ge(exp_done, t + 1)
                v.reciprocal(e_inv[:, :], e_sum[:, :]).then_inc(e_inv_done, 1)
                v.wait_ge(e_inv_done, t + 1)
                v.tensor_scalar(probs[:, :], expd[:, :], e_inv[:, 0:1], None, ALU.mult).then_inc(probs_done, 1)
                v.wait_ge(consts_in, 48)
                v.wait_ge(probs_done, t + 1)
                v.max(top8[:, :], probs[:, :]).then_inc(top8_done, 1)
                v.wait_ge(consts_in, 48)
                v.wait_ge(top8_done, t + 1)
                v.match_replace(out=rest[:, :], in_to_replace=top8[:, :], in_values=probs[:, :],
                                imm_value=-1.0).then_inc(rest_done, 1)
                v.wait_ge(rest_done, t + 1)
                v.scalar_tensor_tensor(chosen[:, :], rest[:, :], 0.0, probs[:, :], ALU.max, ALU.subtract,
                                       accum_out=chosen_sum[:, :]).then_inc(chosen_done, 1)
                v.wait_ge(chosen_done, t + 1)
                v.reciprocal(chosen_inv[:, :], chosen_sum[:, :]).then_inc(chosen_inv_done, 1)
                v.wait_ge(chosen_inv_done, t + 1)
                v.tensor_scalar(gate[:, bass.ds(t, 1), :].rearrange("p a e -> p (a e)"), chosen[:, :], chosen_inv[:, 0:1],
                                1.0 / WS, ALU.mult, ALU.mult).then_inc(gate_done, 1)

            tiles(v, step)

        @block.scalar
        def _(act):
            for n in range(H // PART):
                act.dma_start(acc[:, n * PART:(n + 1) * PART, :],
                              d["wo"][:, n * PART:(n + 1) * PART, :]).then_inc(wo_loaded[n], 16)
            act.dma_start(up_in[:, :, :], d["up"][0]).then_inc(w_loaded, 16)
            act.dma_start(down_in[:, :, :], d["down"][0]).then_inc(w_loaded, 16)
            act.wait_ge(consts_in, 48)
            act.activation(wg_hi[:, :, :], wg_in[:, :, :], ACT.Copy, scale=WS).then_inc(wo_hi_done, 1)
            for n in range(H // PART):
                act.wait_ge(wo_loaded[n], 16)
                act.activation(wo_hi[:, n * PART:(n + 1) * PART, :], acc[:, n * PART:(n + 1) * PART, :], ACT.Copy,
                               scale=WS).then_inc(wo_hi_done, 1)

            act.wait_ge(w_loaded, 32)
            act.activation(up_hi[:, :, :], up_in[:, :, :], ACT.Copy, scale=WS)
            act.activation(down_hi[:, :, :], down_in[:, :, :], ACT.Copy, scale=WS).then_inc(w_hi_done, 1)

            def step(t, n, pair):
                s = n % 2
                act.wait_ge(norm_turned, t + 1)
                act.activation(xt_hi[s][:, :, :], p_norm[s][:, :].rearrange("p (c n) -> p c n", c=DC),
                               ACT.Copy).then_inc(hi_done, 1)
                act.wait_ge(top_bias_done, 2 * t + 2)
                act.activation(expd[:, :], p_logit[:, 0:E], ACT.Exp, bias=top_bias[:, 0:1], scale=1.0 / WS,
                               accum_out=e_sum[:, :]).then_inc(exp_done, 1)

            tiles(act, step)


def expert_phase(nc, d, x_hi, x_lo, acc, gate, first):
    with ExitStack() as ctx:
        sb = lambda name, shape, dt=F32: ctx.enter_context(nc.sbuf_tensor(name, shape, dt))
        ps = lambda name, shape: ctx.enter_context(nc.psum_tensor(name, shape, F32))
        sem = lambda name: ctx.enter_context(nc.semaphore(name))
        FR = F - P
        AHEAD = NT + 1
        up_in = [first[0], sb("up_in1", [P, DC, 2 * F])]
        up_hi = [first[1], sb("up_hi1", [P, DC, 2 * F], F16)]
        up_lo = [first[2], sb("up_lo1", [P, DC, 2 * F], F16)]
        down_in = [first[3], sb("down_in1", [P, 2, D])]
        down_hi = [first[4], sb("down_hi1", [P, 2, D], F16)]
        down_lo = [first[5], sb("down_lo1", [P, 2, D], F16)]
        silu = sb("silu", [P, 2, 512])
        hid = [sb(f"hid_d{i}", [P, 2, 512]) for i in range(2)]
        hid_hi = [sb(f"hid_hi{i}", [P, 512], F16) for i in range(2)]
        hid_lo = [sb(f"hid_lo{i}", [P, 512], F16) for i in range(2)]
        hid_rest = [sb(f"hid_rest{i}", [P, 512], F16) for i in range(2)]
        p_up = [ps(f"p_up{i}", [P, 3, 512]) for i in range(2)]
        p_down = [ps(f"p_down{i}", [P, 512]) for i in range(2)]
        up_loaded = [sem(f"up_loaded{i}") for i in range(2)]
        w_hi_done = sem("d_w_hi_done")
        w_lo_done = sem("d_w_lo_done")
        up_done = sem("up_done")
        silu_done = sem("silu_done")
        hid_done = sem("d_hid_done")
        hid_hi_done = sem("hid_hi_done")
        rest_split = sem("rest_split")
        hid_split = sem("hid_split")
        down_done = sem("down_done")
        added = sem("added")
        stored = sem("stored")
        block = ctx.enter_context(nc.Block())

        def experts(eng, body):
            with eng.Fori(0, E // 2 - 1) as pair:
                for u in range(2):
                    body(pair * 2 + u, u, pair)
            for u in range(2):
                body(E - 2 + u, u, E // 2 - 1)

        def there_is(e):
            return not isinstance(e, int) or e < E

        def following(e, u, b):
            if b + 1 < NB:
                return e, u, b + 1
            return (e + 1, 1 - u, 0) if there_is(e + 1) else None

        @block.sync
        def _(sp):
            def load(e, u):
                sp.wait_ge(w_lo_done, e + 1)
                one = lambda a: a[bass.ds(e, 1)]
                sp.dma_start(up_in[u][:, :, :], one(d["up"]).rearrange("a p c f -> (a p) c f")).then_inc(up_loaded[u], 16)
                sp.dma_start(down_in[u][:, :, :], one(d["down"]).rearrange("a p k n -> (a p) k n")).then_inc(up_loaded[u], 16)

            experts(sp, lambda e, u, pair: load(e + 1, 1 - u) if there_is(e + 1) else None)
            for b in range(NB):
                sp.wait_ge(added, NT * (E - 1) + 4 * (b + 1) + 2)
                sp.dma_start(d["out"][b * 512:(b + 1) * 512, :].rearrange("(t p) n -> p t n", p=P),
                             acc[:, 4 * b:4 * b + 4, :]).then_inc(stored, 16)
            sp.wait_ge(stored, 16 * NB)

        @block.tensor
        def _(pe):
            pe.sem_inc(down_done, AHEAD)

            def up(e, u, b):
                no = NB * e + b
                pe.wait_ge(hid_done, no + 1)
                if b == 0:
                    pe.wait_ge(w_lo_done, e + 3)
                cols = slice(b * 512, (b + 1) * 512)
                for m in range(3):
                    for c in range(DC):
                        for p, (w, xx) in enumerate(((up_hi, x_hi), (up_lo, x_hi), (up_hi, x_lo))):
                            last = pe.matmul(p_up[b % 2][:, m, :], w[u][:, c, m * P:(m + 1) * P], xx[:, c, cols],
                                             start=(c == 0 and p == 0), stop=(c == DC - 1 and p == 2))
                last.then_inc(up_done, 1)

            def down(e, u, b):
                pe.wait_ge(hid_split, NB * e + b + 2)
                for t in range(4):
                    no = NT * e + 4 * b + t
                    pe.wait_ge(added, no + 1)
                    cols = slice(t * P, (t + 1) * P)
                    h0, l0, h1 = hid_hi[b % 2][:, cols], hid_lo[b % 2][:, cols], hid_rest[b % 2]
                    for n, (hh, w) in enumerate((
                            (h0, down_hi[u][:, 0, :]), (h0, down_lo[u][:, 0, :]), (l0, down_hi[u][:, 0, :]),
                            (h1[:, cols], down_hi[u][:, 1, :]), (h1[0:FR, cols], down_lo[u][0:FR, 1, :]))):
                        last = pe.matmul(p_down[t % 2][:, :], hh, w, start=(n == 0), stop=(n == 4))
                    last.then_inc(down_done, 1)

            def body(e, u, pair):
                for b in range(NB):
                    if block_after := following(e, u, b):
                        up(*block_after)
                    down(e, u, b)

            up(0, 0, 0)
            experts(pe, body)

        @block.scalar
        def _(act):
            def split(e, u, pair):
                act.wait_ge(up_loaded[u], 32 * (pair + 1))
                act.wait_ge(down_done, NT * e + 1)
                act.activation(up_hi[u][:, :, :], up_in[u][:, :, :], ACT.Copy, scale=WS)
                act.activation(down_hi[u][:, :, :], down_in[u][:, :, :], ACT.Copy, scale=WS).then_inc(w_hi_done, 1)

            def silu_and_high(e, u, b):
                act.wait_ge(up_done, NB * e + b + 1)
                act.wait_ge(hid_done, NB * e + b + 2)
                act.activation(silu[:, 0, :], p_up[b % 2][:, 0, :], ACT.Silu, scale=1.0 / WS)
                act.activation(silu[0:FR, 1, :], p_up[b % 2][0:FR, 2, :], ACT.Silu, scale=1.0 / WS).then_inc(silu_done, 1)
                act.wait_ge(hid_done, NB * e + b + 3)
                act.activation(hid_hi[b % 2][:, :], hid[b % 2][:, 0, :], ACT.Copy)
                act.activation(hid_rest[b % 2][0:FR, :], hid[b % 2][0:FR, 1, :], ACT.Copy).then_inc(hid_hi_done, 1)

            def body(e, u, pair):
                for b in range(NB):
                    if block_after := following(e, u, b):
                        silu_and_high(*block_after)
                    if b == 1 and there_is(e + 1):
                        split(e + 1, 1 - u, pair)

            silu_and_high(0, 0, 0)
            experts(act, body)

        @block.vector
        def _(v):
            v.sem_inc(hid_done, 2)
            v.sem_inc(w_lo_done, 3)
            v.sem_inc(added, 2)

            def split(e, u):
                v.wait_ge(w_hi_done, e)
                v.scalar_tensor_tensor(up_lo[u][:, :, :], up_in[u][:, :, :], WS, up_hi[u][:, :, :], ALU.mult, ALU.subtract)
                v.scalar_tensor_tensor(down_lo[u][:, :, :], down_in[u][:, :, :], WS, down_hi[u][:, :, :], ALU.mult,
                                       ALU.subtract).then_inc(w_lo_done, 1)

            def multiply(e, u, b):
                v.wait_ge(silu_done, NB * e + b + 1)
                v.scalar_tensor_tensor(hid[b % 2][:, 0, :], p_up[b % 2][:, 1, :], 1.0 / WS, silu[:, 0, :], ALU.mult, ALU.mult)
                v.scalar_tensor_tensor(hid[b % 2][0:FR, 1, :], p_up[b % 2][FR:P, 2, :], 1.0 / WS, silu[0:FR, 1, :],
                                       ALU.mult, ALU.mult).then_inc(hid_done, 1)

            def add(e, tile):
                v.wait_ge(down_done, NT * e + (tile + 1 + AHEAD))
                v.scalar_tensor_tensor(acc[:, tile, :], p_down[tile % 2][:, :], gate[:, tile, bass.ds(e, 1)],
                                       acc[:, tile, :], ALU.mult, ALU.add).then_inc(added, 1)

            def body(e, u, pair):
                for b in range(NB):
                    add(e, 4 * b)
                    add(e, 4 * b + 1)
                    if block_after := following(e, u, b):
                        multiply(*block_after)
                    add(e, 4 * b + 2)
                    add(e, 4 * b + 3)
                    if b == 1 and there_is(e + 1):
                        split(e + 1, 1 - u)

            multiply(0, 0, 0)
            experts(v, body)

        @block.gpsimd
        def _(pool):
            def low(e, u, b):
                pool.wait_ge(hid_split, NB * e + b + 1)
                pool.wait_ge(hid_hi_done, NB * e + b + 1)
                pool.tensor_tensor(hid_rest[b % 2][FR:P, :], hid[b % 2][0:FR, 1, :], hid_rest[b % 2][0:FR, :],
                                   ALU.subtract).then_inc(rest_split, 1)
                pool.wait_ge(rest_split, NB * e + b + 1)
                pool.tensor_tensor(hid_lo[b % 2][:, :], hid[b % 2][:, 0, :], hid_hi[b % 2][:, :],
                                   ALU.subtract).then_inc(hid_split, 1)

            def body(e, u, pair):
                for b in range(NB):
                    if block_after := following(e, u, b):
                        low(*block_after)

            pool.sem_inc(hid_split, 1)
            low(0, 0, 0)
            experts(pool, body)


def build(nc, d):
    with ExitStack() as ctx:
        keep = lambda stack, name, shape, dt=F32: stack.enter_context(nc.sbuf_tensor(name, shape, dt))
        x_hi = keep(ctx, "x_hi", [P, DC, T], F16)
        x_lo = keep(ctx, "x_lo", [P, DC, T], F16)
        with ExitStack() as to_attention:
            early = (
                keep(to_attention, "ident_a", [P, P]),
                keep(to_attention, "mask", [P, P]),
                keep(to_attention, "cos", [P, T]),
                keep(to_attention, "sin", [P, T]),
                keep(to_attention, "bqk", [P, 2, H]),
                [keep(to_attention, f"bv{i}", [P, P]) for i in range(2)],
                keep(to_attention, "w_in", [P, 3, DC, P]),
                keep(to_attention, "w_hi", [P, 3, DC, P], F16),
                keep(to_attention, "w_lo", [P, 3, DC, P], F16),
            )
            embed_phase(nc, d, x_hi, x_lo, early)
            attention_phase(nc, d, x_hi, x_lo, early)
        acc = keep(ctx, "acc", [P, NT, D])
        gate = keep(ctx, "gate", [P, NT, E])
        first = [keep(ctx, f"{name}0", shape, dt) for name, shape, dt in (
            ("up_in", [P, DC, 2 * F], F32), ("up_hi", [P, DC, 2 * F], F16), ("up_lo", [P, DC, 2 * F], F16),
            ("down_in", [P, 2, D], F32), ("down_hi", [P, 2, D], F16), ("down_lo", [P, 2, D], F16))]
        output_phase(nc, d, x_hi, x_lo, acc, gate, first)
        expert_phase(nc, d, x_hi, x_lo, acc, gate, first)


def host_layout(x, emb, lora_A, lora_B, wq, wk, wv, wo, bq, bk, bv, bo, wg, w1, v1, w2):
    import numpy as np
    turn = np.concatenate([np.arange(0, P, 2), np.arange(1, P, 2)])
    chunked = lambda w: w.reshape(H, DC, P, P).transpose(0, 2, 1, 3)
    wqkv = np.stack([chunked(wq[:, :, turn]), chunked(wk[:, :, turn]), chunked(wv)], axis=2)
    inv_freq = np.float32(1.0) / (10000.0 ** (np.arange(0, P, 2) / P)).astype(np.float32)
    freqs = np.arange(T, dtype=np.float32)[None, :] * inv_freq[:, None]
    cos, sin = np.cos(freqs).astype(np.float32), np.sin(freqs).astype(np.float32)
    gain = np.float32(QS / WS)
    padded = lambda w: np.ascontiguousarray(np.concatenate([w, w[:1]]))
    return {
        "idx": np.ascontiguousarray(x.reshape(NT, P).T),
        "emb": emb,
        "lora_at": np.ascontiguousarray(lora_A.T),
        "lora_b": np.ascontiguousarray(lora_B.T),
        "ident": np.eye(P, dtype=np.float32),
        "mask": np.tril(np.ones((P, P), np.float32)),
        "cos": np.concatenate([cos, cos]) * gain,
        "sin": np.concatenate([-sin, sin]) * gain,
        "bqk": np.ascontiguousarray(np.stack([bq[:, turn].T, bk[:, turn].T], axis=1)),
        "wqkv": padded(wqkv),
        "bv": padded(bv),
        "wo": np.ascontiguousarray(wo.transpose(1, 0, 2)),
        "bo": bo.reshape(1, D),
        "wg": np.ascontiguousarray(wg.T.reshape(DC, P, E).transpose(1, 0, 2)),
        "up": np.ascontiguousarray(np.concatenate([w1[:, :, :P], v1[:, :, :P], w1[:, :, P:], v1[:, :, P:]], axis=2)
                                   .reshape(E, DC, P, 2 * F).transpose(0, 2, 1, 3)),
        "down": np.ascontiguousarray(np.stack([w2[:, :P], np.concatenate([w2[:, P:], w2[:, P:]], axis=1)], axis=2)),
    }


def kernel(x, L0_tok_weight, L0_tok_lora_A, L0_tok_lora_B, L0_attn_W_Q, L0_attn_W_K, L0_attn_W_V, L0_attn_W_O, L0_attn_b_Q,
           L0_attn_b_K, L0_attn_b_V, L0_attn_b_O, L0_ffn_wg, L0_ffn_w1, L0_ffn_v1, L0_ffn_w2):
    import concourse.bacc as bacc
    import numpy as np
    from concourse.bass_utils import run_bass_kernel_spmd

    arrays = host_layout(*(np.asarray(a) for a in (
        x, L0_tok_weight, L0_tok_lora_A, L0_tok_lora_B, L0_attn_W_Q, L0_attn_W_K, L0_attn_W_V, L0_attn_W_O, L0_attn_b_Q,
        L0_attn_b_K, L0_attn_b_V, L0_attn_b_O, L0_ffn_wg, L0_ffn_w1, L0_ffn_v1, L0_ffn_w2)))
    arrays = {f"in_{name}": a for name, a in arrays.items()}
    nc = bacc.Bacc("TRN2", target_bir_lowering=False, num_devices=1)
    d = {name[3:]: nc.dram_tensor(name, a.shape, mybir.dt.from_np(a.dtype), kind="ExternalInput").ap()
         for name, a in arrays.items()}
    d["out"] = nc.dram_tensor("out_h", [T, D], F32, kind="ExternalOutput").ap()
    d["h"] = nc.dram_tensor("scratch_h", [T, D], F32).ap()
    d["z"] = nc.dram_tensor("scratch_z", [P, 2 * H, T], F16).ap()
    build(nc, d)
    r = run_bass_kernel_spmd(nc, [arrays], core_ids=[0])
    return r.results[0]["out_h"].reshape(1, T, D)
```
